# Optimizing a Trainium2 kernel written in Bass

```python
import numpy as np
import jax
import jax.numpy as jnp

def _softmax(x, axis=-1):
    return jax.nn.softmax(x, axis=axis)

def _gelu(x):
    return jax.nn.gelu(x, approximate=True)

def _silu(x):
    return jax.nn.silu(x)

def _sigmoid(x):
    return jax.nn.sigmoid(x)

def _layernorm(x, axis=-1, eps=1e-05):
    m = jnp.mean(x, axis=axis, keepdims=True)
    v = jnp.var(x, axis=axis, keepdims=True)
    return (x - m) / jnp.sqrt(v + eps)

def _scatter_add(tgt, idx, src, axis=0):
    return tgt.at[idx].add(src)

def _segment_sum(src, seg, n):
    return jax.ops.segment_sum(src, seg, n)
kernel_name = 'mk_lm_tower_d1_tok_ids512_r4_b547d7'

def setup_inputs(seed: int=0):
    np.random.seed(seed)
    _w = jnp.asarray

    def _rec_inputs():
        import jax
        import jax.numpy as jnp
        _rk = jax.random.key(seed)
        x = jax.random.randint(jax.random.fold_in(_rk, 1), (32, 512), 0, 125, jnp.int32)
        return x
    x = _rec_inputs()

    def _L0_tok_setup():
        import jax, jax.numpy as jnp
        import numpy as np
        QMAX = 127.0
        CTX = 2

        def fake_quant(w):
            scale = jnp.max(jnp.abs(w)) / QMAX
            wq = jnp.round(w / scale) * scale
            return w + jax.lax.stop_gradient(wq - w)
        key = jax.random.key(seed)
        k1, k2, k3 = jax.random.split(key, 3)
        y = jax.random.randint(k1, (64, 512), 0, 125, dtype=jnp.int64)
        emb_weight = jax.random.normal(k2, (125, 128), dtype=jnp.float32)
        conv_weight = jax.random.normal(k3, (128, 1, 2), dtype=jnp.float32)
        return {'y': y, 'emb_weight': emb_weight, 'conv_weight': conv_weight}
    _L0_tok_all = _L0_tok_setup()
    _L0_tok_in = {k: v for k, v in _L0_tok_all.items() if k in ('emb_weight', 'conv_weight')}
    del _L0_tok_all

    def _L0_attn_setup():
        import jax, jax.numpy as jnp
        import numpy as np
        B, S, D = (8, 512, 128)
        key = jax.random.key(seed)
        k1, k2 = jax.random.split(key)
        lstm_out = jax.random.normal(k1, (B, S, D), dtype=jnp.float32)
        limit = float(np.sqrt(6.0 / (D + D)))
        attention_weights = jax.random.uniform(k2, (D, D), dtype=jnp.float32, minval=-limit, maxval=limit)
        return {'lstm_out': lstm_out, 'attention_weights': attention_weights}
    _L0_attn_all = _L0_attn_setup()
    _L0_attn_in = {k: v for k, v in _L0_attn_all.items() if k in ('attention_weights',)}
    del _L0_attn_all

    def _L0_ffn_setup():
        import jax, jax.numpy as jnp
        import numpy as np
        B, C, IN_LEN, OUT_LEN, E, TOP_K, N_I = (1, 2048, 128, 128, 8, 2, 16)
        key = jax.random.key(seed)
        ks = jax.random.split(key, 8)
        w = lambda k, shape, sc=0.02: jax.random.normal(k, shape, dtype=jnp.float32) * sc
        return {'x': jax.random.normal(ks[0], (B, C, IN_LEN), dtype=jnp.float32), 'Ins_tk': jax.random.normal(ks[1], (B, N_I, OUT_LEN), dtype=jnp.float32), 'gate_w': w(ks[2], (IN_LEN, E)), 'expert_w': w(ks[3], (E, IN_LEN, OUT_LEN)), 'expert_b': jnp.zeros((E, OUT_LEN), dtype=jnp.float32), 'gamma_w': w(ks[4], (E, OUT_LEN)), 'beta_w': w(ks[5], (E, OUT_LEN, OUT_LEN)), 'rmod_w': w(ks[6], (OUT_LEN, E))}
    _L0_ffn_all = _L0_ffn_setup()
    _L0_ffn_in = {k: v for k, v in _L0_ffn_all.items() if k in ('Ins_tk', 'gate_w', 'expert_w', 'expert_b', 'gamma_w', 'beta_w', 'rmod_w')}
    del _L0_ffn_all
    return {'x': x, 'L0_tok_emb_weight': _L0_tok_in['emb_weight'], 'L0_tok_conv_weight': _L0_tok_in['conv_weight'], 'L0_attn_attention_weights': _L0_attn_in['attention_weights'], 'L0_ffn_Ins_tk': _L0_ffn_in['Ins_tk'], 'L0_ffn_gate_w': _L0_ffn_in['gate_w'], 'L0_ffn_expert_w': _L0_ffn_in['expert_w'], 'L0_ffn_expert_b': _L0_ffn_in['expert_b'], 'L0_ffn_gamma_w': _L0_ffn_in['gamma_w'], 'L0_ffn_beta_w': _L0_ffn_in['beta_w'], 'L0_ffn_rmod_w': _L0_ffn_in['rmod_w']}

def reference(x, L0_tok_emb_weight, L0_tok_conv_weight, L0_attn_attention_weights, L0_ffn_Ins_tk, L0_ffn_gate_w, L0_ffn_expert_w, L0_ffn_expert_b, L0_ffn_gamma_w, L0_ffn_beta_w, L0_ffn_rmod_w):
    import jax
    import jax.numpy as jnp

    def _L0_tok_ref(y, emb_weight, conv_weight):
        import jax, jax.numpy as jnp
        import numpy as np
        QMAX = 127.0
        CTX = 2

        def fake_quant(w):
            scale = jnp.max(jnp.abs(w)) / QMAX
            wq = jnp.round(w / scale) * scale
            return w + jax.lax.stop_gradient(wq - w)
        w_emb = fake_quant(emb_weight)
        e = w_emb[jnp.clip(y, 0)]
        e = e * (y >= 0)[..., None].astype(e.dtype)
        x = jnp.pad(e, ((0, 0), (CTX - 1, 0), (0, 0)))
        D = conv_weight.shape[0]
        w = fake_quant(conv_weight).transpose(2, 1, 0)
        out = jax.lax.conv_general_dilated(x, w, window_strides=(1,), padding='VALID', feature_group_count=D, dimension_numbers=('NWC', 'WIO', 'NWC'))
        return jax.nn.relu(out)

    def _L0_attn_ref(lstm_out, attention_weights):
        import jax, jax.numpy as jnp
        import numpy as np
        B, S, D = (8, 512, 128)
        proj = jnp.einsum('bsd,de->bse', lstm_out, attention_weights)
        scores = jnp.tanh(jnp.einsum('bsd,btd->bst', proj, lstm_out))
        attn = jax.nn.softmax(scores, axis=-1)
        return jnp.einsum('bst,btd->bsd', attn, lstm_out)

    def _L0_ffn_ref(x, Ins_tk, gate_w, expert_w, expert_b, gamma_w, beta_w, rmod_w):
        import jax, jax.numpy as jnp
        import numpy as np
        B, C, IN_LEN, OUT_LEN, E, TOP_K, N_I = (1, 2048, 128, 128, 8, 2, 16)
        Bx, Cx, L = x.shape
        xf = x.reshape(-1, L)
        ins = Ins_tk[0]
        router_gamma = jnp.mean(ins @ rmod_w, axis=0)
        logits = xf @ gate_w + router_gamma
        probs = jax.nn.softmax(logits.astype(jnp.float32), axis=-1)
        rw, sel = jax.lax.top_k(probs, TOP_K)
        combine = jnp.sum(jax.nn.one_hot(sel, E, dtype=rw.dtype) * rw[..., None], axis=1)
        gam = jnp.mean(ins @ gamma_w.T, axis=0)
        bet = jnp.einsum('nh,ehd->ed', ins, beta_w) / N_I
        eo = jnp.einsum('nl,eld->end', xf, expert_w) + expert_b[:, None, :]
        mod = gam[:, None, None] * eo + bet[:, None, :]
        out = jnp.einsum('ne,end->nd', combine, mod)
        return out.reshape(Bx, Cx, OUT_LEN)
    h = _L0_tok_ref(x, L0_tok_emb_weight, L0_tok_conv_weight)
    h = h + _L0_attn_ref(_layernorm(h, axis=-1), L0_attn_attention_weights)
    h = h + _L0_ffn_ref(_layernorm(h, axis=-1), L0_ffn_Ins_tk, L0_ffn_gate_w, L0_ffn_expert_w, L0_ffn_expert_b, L0_ffn_gamma_w, L0_ffn_beta_w, L0_ffn_rmod_w)
    return h

_drawn_inputs = setup_inputs


def setup_inputs(seed=0):
    import zlib

    import numpy as np

    out = dict(_drawn_inputs(seed))
    spreads = {'L0_ffn_expert_b': (0.0, 0.8)}
    factors = {'L0_ffn_Ins_tk': 4.672,
     'L0_ffn_gate_w': 5.907,
     'L0_ffn_expert_w': 8.0,
     'L0_ffn_gamma_w': 8.0,
     'L0_ffn_beta_w': 5.05,
     'L0_ffn_rmod_w': 8.0}
    for name, (base, spread) in spreads.items():
        noise = np.random.default_rng([zlib.crc32(name.encode()), seed]).standard_normal(out[name].shape)
        drawn = base * np.exp(spread * noise) if base else spread * noise
        out[name] = jnp.asarray(drawn.astype(out[name].dtype))
    for name, factor in factors.items():
        out[name] = (out[name] * factor).astype(out[name].dtype)
    return out
```

```python
import concourse.bass as bass
from concourse import mybir
from contextlib import ExitStack


def tower_kernel(
    nc: bass.Bass,
    tokens: bass.AP,
    emb_weight: bass.AP,
    conv_weight: bass.AP,
    attn_weight: bass.AP,
    instructions: bass.AP,
    gate_weight: bass.AP,
    expert_weight: bass.AP,
    expert_bias: bass.AP,
    gamma_weight: bass.AP,
    beta_weight: bass.AP,
    rmod_weight: bass.AP,
    out: bass.AP,
):
    fp32 = mybir.dt.float32
    fp16 = mybir.dt.float16
    i32 = mybir.dt.int32
    ALU = mybir.AluOpType
    ACT = mybir.ActivationFunctionType
    AX = mybir.AxisListType
    ABSMAX = bass.bass_isa.ReduceOp.absmax

    B, S = tokens.shape
    V, D = emb_weight.shape
    E = gate_weight.shape[1]
    NI = instructions.shape[1]
    P = 128
    J = S // P
    HE = E // 2
    EPS = 1e-5
    QMAX = 127.0
    ROUND = 12582912.0
    LIFT = 1024.0
    TINY = 1e-30
    EXPONENT_BITS = 0x7F800000
    PROJ_SCALE = 2.0 ** -14
    MASKED = -1e30

    y_rows = tokens
    out_rows = out.rearrange("b (p j) d -> b p j d", j=J)

    ctx = ExitStack()
    with ctx:
        def sb(name, shape, dt):
            return ctx.enter_context(nc.sbuf_tensor(name, shape, dt))

        def sem(name):
            return ctx.enter_context(nc.semaphore(name))

        emb = sb("emb", [P, D], fp32)
        conv = sb("conv", [P, D * 2], fp32)
        conv_q = sb("conv_q", [P, D * 2], fp32)
        emb_q = sb("emb_q", [P, D], fp32)
        table = sb("table", [P, 2, D], fp32)
        table_hi = sb("table_hi", [P, 2, D], fp16)
        table_lo = sb("table_lo", [P, 2, D], fp16)
        attn_w = sb("attn_w", [P, D], fp32)
        attn_hi = sb("attn_hi", [P, D], fp16)
        attn_lo = sb("attn_lo", [P, D], fp16)
        gate_w = sb("gate_w", [P, E], fp32)
        gate_hi = sb("gate_hi", [P, E], fp16)
        gate_lo = sb("gate_lo", [P, E], fp16)
        expert_w = sb("expert_w", [P, E, D], fp32)
        expert_hi = sb("expert_hi", [P, E, D], fp16)
        expert_lo = sb("expert_lo", [P, E, D], fp16)
        expert_b = sb("expert_b", [P, E, D], fp32)
        beta_w = sb("beta_w", [P, E, D], fp32)
        bias_all = sb("bias_all", [P, E, D], fp32)
        gamma_w = sb("gamma_w", [E, D], fp32)
        gamma_t = sb("gamma_t", [P, E], fp32)
        rmod_w = sb("rmod_w", [P, E], fp32)
        ins_w = sb("ins_w", [NI, D], fp32)
        ins_mean = sb("ins_mean", [P, P], fp32)
        sixteenth = sb("sixteenth", [NI, P], fp32)
        router_gamma = sb("router_gamma", [P, E], fp32)
        gam = sb("gam", [P, E], fp32)
        bias_row = sb("bias_row", [P, D], fp32)
        bias_hi = sb("bias_hi", [P, D], fp16)
        bias_lo = sb("bias_lo", [P, D], fp16)
        bias_blocks = sb("bias_blocks", [P, J, D], fp16)
        row_expert = sb("row_expert", [P, E, P // E], fp32)
        row_is = sb("row_is", [P, E], fp32)
        lo_rows = sb("lo_rows", [P, J, 16], fp32)
        is_lo = sb("is_lo", [P, 1], fp32)
        is_hi = sb("is_hi", [P, 1], fp32)
        amax = sb("amax", [P, 4], fp32)
        amax_all = sb("amax_all", [P, 4], fp32)
        amax2 = sb("amax2", [P, 2], fp32)
        amax2_all = sb("amax2_all", [P, 2], fp32)
        step_of = sb("step_of", [P, 6], fp32)
        inv_step = sb("inv_step", [P, 6], fp32)
        unscale = sb("unscale", [P, 6], fp32)
        h_scale = sb("h_scale", [P, 1], fp32)
        vocab_id = sb("vocab_id", [P, 1], fp32)
        first_wins = sb("first_wins", [P, J, E], fp32)
        minus_half = sb("minus_half", [P, J], fp32)
        idle = sb("idle", [P, 1], fp32)
        eps = sb("eps", [P, J], fp32)
        lift = sb("lift", [P, J], fp32)
        ident = sb("ident", [P, P], fp32)
        ident16 = sb("ident16", [P, P], fp16)

        y_bc = [sb(f"y_bc{n}", [P, S], i32) for n in range(2)]
        onehot = [sb(f"onehot{n}", [P, S + 1], fp16) for n in range(2)]
        h1 = [sb(f"h1_{n}", [P, J, D], fp32) for n in range(2)]
        u1 = [sb(f"u1_{n}", [P, J, D + 4], fp32) for n in range(2)]
        stats1 = sb("stats1", [P, J, 6], fp32)
        mv1 = sb("mv1", [P, J, 2], fp32)
        var1 = sb("var1", [P, J], fp32)
        rstd1 = sb("rstd1", [P, J], fp32)
        uT_hi = sb("uT_hi", [P, S], fp16)
        uT_lo = sb("uT_lo", [P, S], fp16)
        pT_hi = sb("pT_hi", [P, S], fp16)
        pT_lo = sb("pT_lo", [P, S], fp16)
        th = [sb(f"th{n}", [P, S], fp32) for n in range(2)]
        probs = sb("probs", [P, J, S], fp32)
        inv_z = sb("inv_z", [P, 2, 2], fp32)
        h2 = [sb(f"h2_{n}", [P, J, D], fp32) for n in range(2)]
        stats2 = sb("stats2", [P, J, 6], fp32)
        mv2 = sb("mv2", [P, J, 2], fp32)
        var2 = sb("var2", [P, J], fp32)
        rstd2 = sb("rstd2", [P, J], fp32)
        u2 = sb("u2", [P, J, D], fp32)
        u2T_hi = [sb(f"u2T_hi{n}", [P, S], fp16) for n in range(2)]
        u2T_lo = [sb(f"u2T_lo{n}", [P, S], fp16) for n in range(2)]
        logits = sb("logits", [P, J, E], fp32)
        top1 = sb("top1", [P, J], fp32)
        below = sb("below", [P, J, E], fp32)
        expo = sb("expo", [P, J, E], fp32)
        expo_sum = sb("expo_sum", [P, J], fp32)
        expo_inv = sb("expo_inv", [P, J], fp32)
        inv_lift = sb("inv_lift", [P, J], fp32)
        rank1 = sb("rank1", [P, J, E], fp32)
        best1 = sb("best1", [P, J], fp32)
        pick1 = sb("pick1", [P, J, E], fp32)
        rest = sb("rest", [P, J, E], fp32)
        top2 = sb("top2", [P, J], fp32)
        tied2 = sb("tied2", [P, J, E], fp32)
        rank2 = sb("rank2", [P, J, E], fp32)
        best2 = sb("best2", [P, J], fp32)
        pick2 = sb("pick2", [P, J, E], fp32)
        picks = sb("picks", [P, J, E], fp32)
        picked = sb("picked", [P, J, E], fp32)
        combine = sb("combine", [P, J, E], fp32)
        combine_y = [sb(f"combine_y{n}", [P, J, E], fp32) for n in range(2)]
        cpack = sb("cpack", [P, J, 32], fp16)
        cT = sb("cT", [P, P], fp16)
        acc = [sb(f"acc{n}", [P, J, D], fp32) for n in range(2)]
        y_odd = [sb(f"y_odd{n}", [P, HE, D], fp32) for n in range(2)]
        prod = sb("prod", [P, HE, D], fp32)
        sum2 = sb("sum2", [P, 2, D], fp32)
        sum1 = sb("sum1", [P, D], fp32)
        out_sb = [sb(f"out_sb{n}", [P, J, D], fp32) for n in range(2)]

        def bank(name):
            return ctx.enter_context(nc.psum_tensor(name, [P, 512], fp32))

        ps_s = [bank(f"ps_s{n}") for n in range(2)]
        ps_y = [bank(f"ps_y{n}") for n in range(2)]
        ps_o = [bank(f"ps_o{n}") for n in range(2)]
        ps_a = bank("ps_a")
        ps_b = bank("ps_b")
        O_STEP = 256

        loaded = {n: sem(f"loaded_{n}") for n in ("emb", "conv", "attn", "gate", "expert", "bias", "beta", "small")}
        amax_zeroed = sem("amax_zeroed")
        consts_made = sem("consts_made")
        amax_spread = sem("amax_spread")
        pool_setup = sem("pool_setup")
        dve_setup = sem("dve_setup")
        amax_found = sem("amax_found")
        means_out = sem("means_out")
        means_mm = sem("means_mm")
        weights_ready = sem("weights_ready")
        y_loaded = [sem(f"y_loaded{n}") for n in range(2)]
        out_stored = [sem(f"out_stored{n}") for n in range(2)]
        onehot_ready = sem("onehot_ready")
        h_mm = sem("h_mm")
        h_relu = sem("h_relu")
        st1_done = sem("st1_done")
        mv1_done = sem("mv1_done")
        var1_done = sem("var1_done")
        rstd1_done = sem("rstd1_done")
        u1_done = sem("u1_done")
        t_mm = sem("t_mm")
        uthi_done = sem("uthi_done")
        utlo_done = sem("utlo_done")
        p_mm = sem("p_mm")
        phi_done = sem("phi_done")
        plo_done = sem("plo_done")
        s_mm = sem("s_mm")
        tanh_done = sem("tanh_done")
        exp_done = sem("exp_done")
        o_mm = sem("o_mm")
        invz_done = sem("invz_done")
        h2_done = sem("h2_done")
        st2_done = sem("st2_done")
        mv2_done = sem("mv2_done")
        var2_done = sem("var2_done")
        rstd2_done = sem("rstd2_done")
        u2_done = sem("u2_done")
        u2_mm = sem("u2_mm")
        u2hi_done = sem("u2hi_done")
        u2lo_done = sem("u2lo_done")
        g_mm = sem("g_mm")
        route = sem("route")
        gexp_done = sem("gexp_done")
        route_p = sem("route_p")
        zsum_done = sem("zsum_done")
        inv_done = sem("inv_done")
        ct_mm = sem("ct_mm")
        ct_done = sem("ct_done")
        b_mm = sem("b_mm")
        acc_init = sem("acc_init")
        y_even_mm = sem("y_even_mm")
        y_odd_mm = sem("y_odd_mm")
        acc_step = sem("acc_step")
        y_odd_done = sem("y_odd_done")
        y_sum = sem("y_sum")
        fin_done = sem("fin_done")

        RD = 12
        RP = 8

        LOOP_FROM, LOOP_TO = 4, B - 2

        def has(i, n):
            return i is None or 0 <= i + n < B

        def run(eng, body):
            for i in range(-2, LOOP_FROM):
                body(i, i, i % 2)
            with eng.Fori(LOOP_FROM // 2, LOOP_TO // 2) as pair:
                for half in range(2):
                    body(None, pair * 2 + half, half)
            for i in range(LOOP_TO, B + 2):
                body(i, i, i % 2)

        def late(i, b, n=1):
            return i is None or b >= n

        block = ctx.enter_context(nc.Block())

        @block.sync
        def _(sp):
            sp.dma_start(emb[0:V, :], emb_weight).then_inc(loaded["emb"], 16)
            sp.dma_start(conv[:, :], conv_weight.rearrange("d o k -> (d o k)").partition_broadcast(P))\
              .then_inc(loaded["conv"], 16)
            sp.dma_start(y_bc[0][0:V, :], y_rows[0, :].partition_broadcast(V)).then_inc(y_loaded[0], 16)
            sp.dma_start(y_bc[1][0:V, :], y_rows[1, :].partition_broadcast(V)).then_inc(y_loaded[1], 16)
            sp.dma_start(attn_w[:, :], attn_weight).then_inc(loaded["attn"], 16)
            sp.dma_start(ins_w[:, :], instructions[0, :, :]).then_inc(loaded["small"], 16)
            sp.dma_start(gamma_w[:, :], gamma_weight).then_inc(loaded["small"], 16)
            sp.dma_start(rmod_w[:, :], rmod_weight).then_inc(loaded["small"], 16)
            sp.dma_start(gate_w[:, :], gate_weight).then_inc(loaded["gate"], 16)
            sp.dma_start(expert_w[:, :, :], expert_weight.rearrange("e l d -> l e d")).then_inc(loaded["expert"], 16)
            sp.dma_start(beta_w[:, :, :], beta_weight.rearrange("e h d -> h e d")).then_inc(loaded["beta"], 16)
            sp.dma_start(expert_b[:, :, :].rearrange("p e d -> p (e d)"),
                         expert_bias.rearrange("e d -> (e d)").partition_broadcast(P)).then_inc(loaded["bias"], 16)

            def body(i, ri, par):
                if has(i, 2) and (i is None or i >= 0):
                    sp.wait_ge(onehot_ready, ri + 1)
                    sp.dma_start(y_bc[par][0:V, :], y_rows[ri + 2, :].partition_broadcast(V))\
                      .then_inc(y_loaded[par], 16)
                if has(i, -2):
                    sp.wait_ge(fin_done, (ri - 2) * J + J)
                    sp.dma_start(out_rows[ri - 2, :, :, :], out_sb[par][:, :, :]).then_inc(out_stored[par], 16)

            run(sp, body)
            for n in range(2):
                sp.wait_ge(out_stored[n], 16 * (B // 2))

        @block.tensor
        def _(pe):
            pe.wait_ge(loaded["small"], 48)
            pe.wait_ge(consts_made, 1)
            nc.tensor.matmul(ps_a[:, 0:P], ins_w[:, :], sixteenth[:, :], start=True, stop=True).then_inc(means_mm, 1)
            nc.tensor.transpose(ps_b[:, 0:E], gamma_w[:, :], ident[0:E, 0:E]).then_inc(means_mm, 1)
            pe.wait_ge(means_out, 2)
            nc.tensor.matmul(ps_a[:, 0:E], ins_mean[:, :], rmod_w[:, :], start=True, stop=True)
            nc.tensor.matmul(ps_a[:, E:2 * E], ins_mean[:, :], gamma_t[:, :], start=True, stop=True).then_inc(means_mm, 1)
            pe.wait_ge(loaded["beta"], 16)
            for n in range(2):
                nc.tensor.matmul(ps_y[n][:, :], ins_mean[:, :], beta_w[:, n * HE:(n + 1) * HE, :],
                                 start=True, stop=True).then_inc(means_mm, 1)

            def body(i, ri, par):
                nxt = 1 - par

                def scores(t):
                    b = ri
                    if t == 0:
                        pe.wait_ge(plo_done, b + 1)
                    if t >= 2 or late(i, b):
                        pe.wait_ge(tanh_done, b * J + t - 1)
                    for n, (a, c) in enumerate(((uT_hi, pT_hi), (uT_hi, pT_lo), (uT_lo, pT_hi))):
                        last = nc.tensor.matmul(ps_s[t % 2][:, :], a[:, t * P:(t + 1) * P], c[:, :],
                                                start=(n == 0), stop=(n == 2))
                    last.then_inc(s_mm, 1)

                def attend(s):
                    b = ri
                    if s == 0:
                        pe.wait_ge(exp_done, b * J + J)
                    if s % 2 == 0 and late(i, b):
                        pe.wait_ge(h2_done, b * 2 - 1 + s // 2)
                    o = ps_o[s // 2][:, (s % 2) * O_STEP:(s % 2) * O_STEP + D + 1]
                    for t in range(J):
                        last = nc.tensor.matmul(o, probs[:, t, s * P:(s + 1) * P], u1[par][:, t, 0:D + 1],
                                                start=(t == 0), stop=(t == J - 1))
                    if s % 2:
                        last.then_inc(o_mm, 1)

                def embed():
                    b = ri + 1
                    pe.wait_ge(onehot_ready, b + 1)
                    if late(i, b):
                        pe.wait_ge(plo_done, b)
                    oh = onehot[nxt]
                    for j in range(J):
                        n = 0
                        for tap in range(2):
                            toks = oh[0:V, tap + j:tap + j + J * (P - 1) + 1:J]
                            for part in (table_hi, table_lo):
                                last = nc.tensor.matmul(ps_a[:, j * D:(j + 1) * D], toks, part[0:V, tap, :],
                                                        start=(n == 0), stop=(n == 3))
                                n += 1
                    last.then_inc(h_mm, 1)

                def turn_u1():
                    pe.wait_ge(u1_done, ri + 2)
                    for j in range(J):
                        last = nc.tensor.transpose(ps_a[:, j * P:(j + 1) * P], u1[nxt][:, j, 0:D], ident[:, :])
                    last.then_inc(t_mm, 1)

                def project():
                    pe.wait_ge(utlo_done, ri + 2)
                    for n, (a, c) in enumerate(((attn_hi, uT_hi), (attn_hi, uT_lo), (attn_lo, uT_hi))):
                        last = nc.tensor.matmul(ps_a[:, :], a[:, :], c[:, :], start=(n == 0), stop=(n == 2))
                    last.then_inc(p_mm, 1)

                def turn_u2():
                    b = ri - 1
                    pe.wait_ge(u2_done, b + 1)
                    if late(i, b):
                        pe.wait_ge(acc_init, b)
                    for j in range(J):
                        last = nc.tensor.transpose(ps_b[:, j * P:(j + 1) * P], u2[:, j, :], ident[:, :])
                    last.then_inc(u2_mm, 1)

                def gate():
                    b = ri - 1
                    pe.wait_ge(u2lo_done, b + 1)
                    for j in range(J):
                        rows = slice(j * P, (j + 1) * P)
                        for n, (a, c) in enumerate(((u2T_hi, gate_hi), (u2T_hi, gate_lo), (u2T_lo, gate_hi))):
                            last = nc.tensor.matmul(ps_b[:, j * E:(j + 1) * E], a[nxt][:, rows], c[:, :],
                                                    start=(n == 0), stop=(n == 2))
                    last.then_inc(g_mm, 1)

                def turn_combine():
                    b = ri - 1
                    pe.wait_ge(route_p, b * RP + 7)
                    nc.tensor.transpose(ps_b[:, 0:P // 2].bitcast(fp16), cpack[:, :, :].rearrange("p j c -> p (j c)"),
                                        ident16[:, :]).then_inc(ct_mm, 1)

                def bias_rows():
                    b = ri - 1
                    pe.wait_ge(ct_done, b + 1)
                    nc.tensor.matmul(ps_b[:, :], cT[:, :], bias_blocks[:, :, :], start=True, stop=True)\
                      .then_inc(b_mm, 1)

                def experts(k, back):
                    b = ri - back
                    q = par if back == 2 else nxt
                    j, half = k // 2, k % 2
                    if j > 0 or late(i, b):
                        if half:
                            pe.wait_ge(y_odd_done, b * J + j)
                        else:
                            pe.wait_ge(acc_step, (b * J + j) * HE)
                    rows = slice(j * P, (j + 1) * P)
                    es = slice(half * HE, (half + 1) * HE)
                    for n, (a, c) in enumerate(((u2T_hi, expert_hi), (u2T_hi, expert_lo), (u2T_lo, expert_hi))):
                        last = nc.tensor.matmul(ps_y[half][:, :], a[q][:, rows], c[:, es, :],
                                                start=(n == 0), stop=(n == 2))
                    last.then_inc(y_odd_mm if half else y_even_mm, 1)

                now, after, e1, e2 = has(i, 0), has(i, 1), has(i, -1), has(i, -2)
                if now:
                    scores(0)
                if e2:
                    experts(3, 2)
                if now:
                    scores(1)
                if e2:
                    experts(4, 2)
                if e1:
                    turn_u2()
                if now:
                    scores(2)
                if e2:
                    experts(5, 2)
                if e1:
                    gate()
                if now:
                    scores(3)
                if e2:
                    experts(6, 2)
                if after:
                    embed()
                if e2:
                    experts(7, 2)
                if now:
                    attend(0)
                if e1:
                    turn_combine()
                if now:
                    attend(1)
                if e1:
                    bias_rows()
                    experts(0, 1)
                if after:
                    turn_u1()
                if now:
                    attend(2)
                if e1:
                    experts(1, 1)
                if after:
                    project()
                if now:
                    attend(3)
                if e1:
                    experts(2, 1)

            pe.wait_ge(weights_ready, 1)
            run(pe, body)

        @block.scalar
        def _(act):
            act.wait_ge(means_mm, 1)
            nc.scalar.activation(ins_mean[:, :], ps_a[:, 0:P], ACT.Copy).then_inc(means_out, 1)
            act.wait_ge(means_mm, 2)
            nc.scalar.activation(gamma_t[:, :], ps_b[:, 0:E], ACT.Copy).then_inc(means_out, 1)
            act.wait_ge(weights_ready, 1)

            def body(i, ri, par):
                nxt = 1 - par

                def tanh(t):
                    act.wait_ge(s_mm, ri * J + t + 1)
                    if t >= 2 or late(i, ri):
                        act.wait_ge(exp_done, ri * J + t - 1)
                    nc.scalar.activation(th[t % 2][:, :], ps_s[t % 2][:, :], ACT.Tanh, scale=unscale[:, 2:3])\
                      .then_inc(tanh_done, 1)

                def exp(t):
                    act.wait_ge(tanh_done, ri * J + t + 1)
                    if t == 0 and late(i, ri):
                        act.wait_ge(o_mm, ri * 2)
                    nc.scalar.activation(probs[:, t, :], th[t % 2][:, :], ACT.Exp).then_inc(exp_done, 1)

                def relu():
                    b = ri + 1
                    act.wait_ge(h_mm, b + 1)
                    if late(i, b, 2):
                        act.wait_ge(h2_done, (b - 2) * 2 + 2)
                    nc.scalar.activation(h1[nxt][:, :, :], ps_a[:, :].rearrange("p (j d) -> p j d", j=J), ACT.Relu,
                                         scale=h_scale[:, 0:1]).then_inc(h_relu, 1)

                def u1_hi():
                    act.wait_ge(t_mm, ri + 2)
                    if has(i, 0):
                        act.wait_ge(s_mm, ri * J + J)
                    nc.scalar.activation(uT_hi[:, :], ps_a[:, :], ACT.Copy, scale=LIFT).then_inc(uthi_done, 1)

                def p_hi():
                    act.wait_ge(p_mm, ri + 2)
                    nc.scalar.activation(pT_hi[:, :], ps_a[:, :], ACT.Copy, scale=PROJ_SCALE).then_inc(phi_done, 1)

                def u2_hi():
                    b = ri - 1
                    act.wait_ge(u2_mm, b + 1)
                    if late(i, b, 2):
                        act.wait_ge(y_odd_mm, (b - 1) * J)
                    nc.scalar.activation(u2T_hi[nxt][:, :], ps_b[:, :], ACT.Copy, scale=LIFT).then_inc(u2hi_done, 1)

                def gate_exp():
                    b = ri - 1
                    act.wait_ge(route, b * RD + 3)
                    nc.scalar.activation(expo[:, :, :], below[:, :, :], ACT.Exp).then_inc(gexp_done, 1)

                def c_out():
                    b = ri - 1
                    act.wait_ge(ct_mm, b + 1)
                    if late(i, b):
                        act.wait_ge(b_mm, b)
                    nc.scalar.activation(cT[:, :], ps_b[:, 0:P // 2].bitcast(fp16), ACT.Copy).then_inc(ct_done, 1)

                def y_out(j, back):
                    b = ri - back
                    act.wait_ge(y_odd_mm, b * J + j + 1)
                    if j >= 2 or late(i, b):
                        act.wait_ge(y_sum, (b * J + j - 1) * 3 - 2)
                    nc.scalar.activation(y_odd[j % 2][:, :, :], ps_y[1][:, :].rearrange("p (e d) -> p e d", e=HE),
                                         ACT.Copy).then_inc(y_odd_done, 1)

                now, after, e1, e2 = has(i, 0), has(i, 1), has(i, -1), has(i, -2)
                if now:
                    tanh(0)
                if e2:
                    y_out(1, 2)
                if now:
                    exp(0)
                    tanh(1)
                    exp(1)
                if e1:
                    u2_hi()
                if now:
                    tanh(2)
                if e2:
                    y_out(2, 2)
                if now:
                    exp(2)
                if e1:
                    gate_exp()
                if now:
                    tanh(3)
                    exp(3)
                if after:
                    relu()
                if e2:
                    y_out(3, 2)
                if e1:
                    c_out()
                if after:
                    u1_hi()
                if e1:
                    y_out(0, 1)
                if after:
                    p_hi()

            run(act, body)

        @block.vector
        def _(dve):
            count = [0]

            def link(ins):
                count[0] += 1
                ins.then_inc(dve_setup, 1)
                dve.wait_ge(dve_setup, count[0])

            for n, (name, ap) in enumerate((("emb", emb[0:V, :]), ("conv", conv[:, :]), ("attn", attn_w[:, :]),
                                            ("gate", gate_w[:, :]))):
                if n == 0:
                    dve.wait_ge(amax_zeroed, 1)
                dve.wait_ge(loaded[name], 16)
                nc.vector.tensor_reduce(amax[0:ap.shape[0], n:n + 1], ap, AX.X, ALU.max,
                                        apply_absolute_value=True).then_inc(amax_found, 1)
            dve.wait_ge(amax_spread, 1)
            link(nc.vector.tensor_scalar(step_of[:, 0:2], amax_all[:, 0:2], 1.0 / QMAX, None, ALU.mult))
            link(nc.vector.reciprocal(inv_step[:, 0:2], step_of[:, 0:2]))
            link(nc.vector.tensor_tensor(h_scale[:, :], step_of[:, 0:1], step_of[:, 1:2], ALU.mult))
            link(nc.vector.tensor_scalar(conv_q[:, :], conv[:, :], inv_step[:, 1:2], ROUND, ALU.mult, ALU.add))
            link(nc.vector.tensor_scalar(conv_q[:, :], conv_q[:, :], ROUND, None, ALU.subtract))
            link(nc.vector.tensor_scalar(emb_q[0:V, :], emb[0:V, :], inv_step[0:V, 0:1], ROUND, ALU.mult, ALU.add))
            taps = conv_q[:, :].rearrange("p (d k) -> p k d", k=2)
            for k in range(2):
                link(nc.vector.scalar_tensor_tensor(table[0:V, k, :], emb_q[0:V, :], ROUND, taps[0:V, k, :],
                                                    ALU.subtract, ALU.mult))
            link(nc.vector.tensor_copy(table_hi[0:V, :, :], table[0:V, :, :]))
            link(nc.vector.tensor_tensor(table_lo[0:V, :, :], table[0:V, :, :], table_hi[0:V, :, :], ALU.subtract))

            def power(src, n):
                w = src.shape[1]
                link(nc.vector.tensor_scalar(step_of[:, n:n + w], src, TINY, None, ALU.max))
                link(nc.vector.tensor_scalar(step_of[:, n:n + w].bitcast(i32), step_of[:, n:n + w].bitcast(i32),
                                             EXPONENT_BITS, None, ALU.bitwise_and))
                link(nc.vector.reciprocal(inv_step[:, n:n + w], step_of[:, n:n + w]))
                link(nc.vector.tensor_scalar(inv_step[:, n:n + w], inv_step[:, n:n + w], LIFT, None, ALU.mult))

            def split(hi, lo, ap, scale):
                link(nc.vector.tensor_scalar(ap, ap, scale, None, ALU.mult))
                link(nc.vector.tensor_copy(hi, ap))
                link(nc.vector.tensor_tensor(lo, ap, hi, ALU.subtract))

            power(amax_all[:, 2:4], 2)
            link(nc.vector.tensor_scalar(unscale[:, 2:3], step_of[:, 2:3], 1.0 / (LIFT * LIFT * LIFT * PROJ_SCALE),
                                         None, ALU.mult))
            link(nc.vector.tensor_scalar(unscale[:, 3:4], step_of[:, 3:4], 1.0 / (LIFT * LIFT), None, ALU.mult))
            split(attn_hi[:, :], attn_lo[:, :], attn_w[:, :], inv_step[:, 2:3])
            split(gate_hi[:, :], gate_lo[:, :], gate_w[:, :], inv_step[:, 3:4])
            dve.wait_ge(means_mm, 3)
            link(nc.vector.tensor_copy(router_gamma[:, :], ps_a[:, 0:E]))
            link(nc.vector.tensor_copy(gam[:, :], ps_a[:, E:2 * E]))
            dve.wait_ge(loaded["expert"], 16)
            dve.wait_ge(loaded["bias"], 16)
            for e in range(E):
                link(nc.vector.tensor_scalar(expert_w[:, e, :], expert_w[:, e, :], gam[:, e:e + 1], None, ALU.mult))
            dve.wait_ge(means_mm, 5)
            for e in range(E):
                link(nc.vector.scalar_tensor_tensor(bias_all[:, e, :], expert_b[:, e, :], gam[:, e:e + 1],
                                                    ps_y[e // HE][:, (e % HE) * D:(e % HE + 1) * D],
                                                    ALU.mult, ALU.add))
            dve.wait_ge(consts_made, 2)
            link(nc.vector.tensor_reduce(row_is[:, :], row_expert[:, :, :], AX.X, ALU.max))
            link(nc.vector.tensor_reduce(is_lo[:, :], lo_rows[:, :, :], AX.XY, ALU.max))
            link(nc.vector.tensor_scalar(is_hi[:, :], is_lo[:, :], -1.0, 1.0, ALU.mult, ALU.add))
            link(nc.vector.tensor_scalar(bias_row[:, :], bias_all[:, 0, :], row_is[:, 0:1], None, ALU.mult))
            for e in range(1, E):
                link(nc.vector.scalar_tensor_tensor(bias_row[:, :], bias_all[:, e, :], row_is[:, e:e + 1],
                                                    bias_row[:, :], ALU.mult, ALU.add))
            nc.vector.tensor_reduce(amax2[:, 0:1], expert_w[:, :, :], AX.XY, ALU.max,
                                    apply_absolute_value=True).then_inc(amax_found, 1)
            nc.vector.tensor_reduce(amax2[:, 1:2], bias_row[:, :], AX.X, ALU.max,
                                    apply_absolute_value=True).then_inc(amax_found, 1)
            dve.wait_ge(amax_spread, 2)
            power(amax2_all[:, :], 4)
            link(nc.vector.tensor_scalar(unscale[:, 4:5], step_of[:, 4:5], 1.0 / (LIFT * LIFT * LIFT), None, ALU.mult))
            link(nc.vector.tensor_scalar(unscale[:, 5:6], step_of[:, 5:6], 1.0 / (LIFT * LIFT), None, ALU.mult))
            split(expert_hi[:, :, :], expert_lo[:, :, :], expert_w[:, :, :], inv_step[:, 4:5])
            split(bias_hi[:, :], bias_lo[:, :], bias_row[:, :], inv_step[:, 5:6])
            link(nc.vector.tensor_scalar(bias_hi[:, :], bias_hi[:, :], is_hi[:, 0:1], None, ALU.mult))
            link(nc.vector.scalar_tensor_tensor(bias_hi[:, :], bias_lo[:, :], is_lo[:, 0:1], bias_hi[:, :],
                                                ALU.mult, ALU.add))
            for j in range(J):
                rows = slice(32 * j, 32 * (j + 1))
                last = nc.vector.tensor_copy(bias_blocks[rows, j, :], bias_hi[rows, :])
                if j < J - 1:
                    link(last)
            last.then_inc(weights_ready, 1)

            def body(i, ri, par):
                nxt = 1 - par

                def moments(h, stats, mv, js, st_sem, mv_sem, at):
                    for j in js:
                        last = nc.vector.bn_stats(stats[:, j, :], h[:, j, :])
                    last.then_inc(st_sem, 1)
                    dve.wait_ge(st_sem, at)
                    nc.vector.memset(idle[:, :], 0.0)
                    for j in js:
                        last = nc.vector.bn_aggr(mv[:, j, :], stats[:, j, :])
                    last.then_inc(mv_sem, 1)

                def one_hot():
                    b = ri + 2
                    dve.wait_ge(y_loaded[par], 8 * (ri + 2 - par) + 16)
                    if late(i, b, 2):
                        dve.wait_ge(h_mm, b - 1)
                    nc.vector.tensor_scalar(onehot[par][0:V, 1:S + 1], y_bc[par][0:V, :], float(V - 1),
                                            vocab_id[0:V, 0:1], ALU.min, ALU.is_equal).then_inc(onehot_ready, 1)

                def stats_1():
                    b = ri + 1
                    dve.wait_ge(h_relu, b + 1)
                    moments(h1[nxt], stats1, mv1, range(J), st1_done, mv1_done, b + 1)

                def norm_1():
                    b = ri + 1
                    dve.wait_ge(rstd1_done, b + 1)
                    if late(i, b, 2):
                        dve.wait_ge(o_mm, (b - 2) * 2 + 2)
                    for j in range(J):
                        last = nc.vector.tensor_scalar(u1[nxt][:, j, 0:D], h1[nxt][:, j, :], mv1[:, j, 0:1],
                                                       rstd1[:, j:j + 1], ALU.subtract, ALU.mult)
                    last.then_inc(u1_done, 1)

                def u1_lo():
                    dve.wait_ge(uthi_done, ri + 2)
                    nc.vector.scalar_tensor_tensor(uT_lo[:, :], ps_a[:, :], LIFT, uT_hi[:, :], ALU.mult, ALU.subtract).then_inc(utlo_done, 1)

                def p_lo():
                    dve.wait_ge(phi_done, ri + 2)
                    nc.vector.scalar_tensor_tensor(pT_lo[:, :], ps_a[:, :], PROJ_SCALE, pT_hi[:, :],
                                                   ALU.mult, ALU.subtract).then_inc(plo_done, 1)

                def residual(o):
                    b = ri
                    dve.wait_ge(o_mm, b * 2 + o + 1)
                    pair = ps_o[o][:, :].rearrange("p (s c) -> p s c", s=2)
                    nc.vector.reciprocal(inv_z[:, o, :], pair[:, :, D]).then_inc(invz_done, 1)
                    dve.wait_ge(invz_done, b * 2 + o + 1)
                    for n in range(2):
                        j = 2 * o + n
                        last = nc.vector.scalar_tensor_tensor(h2[par][:, j, :], pair[:, n, 0:D], inv_z[:, o, n:n + 1],
                                                              h1[par][:, j, :], ALU.mult, ALU.add)
                    last.then_inc(h2_done, 1)
                    dve.wait_ge(h2_done, b * 2 + o + 1)
                    moments(h2[par], stats2, mv2, range(2 * o, 2 * o + 2), st2_done, mv2_done, b * 2 + o + 1)

                def norm_2():
                    b = ri - 1
                    dve.wait_ge(rstd2_done, b + 1)
                    if late(i, b):
                        dve.wait_ge(u2_mm, b)
                    for j in range(J):
                        last = nc.vector.tensor_scalar(u2[:, j, :], h2[nxt][:, j, :], mv2[:, j, 0:1],
                                                       rstd2[:, j:j + 1], ALU.subtract, ALU.mult)
                    last.then_inc(u2_done, 1)

                def u2_lo():
                    dve.wait_ge(u2hi_done, ri)
                    nc.vector.scalar_tensor_tensor(u2T_lo[nxt][:, :], ps_b[:, :], LIFT, u2T_hi[nxt][:, :], ALU.mult,
                                                   ALU.subtract)\
                      .then_inc(u2lo_done, 1)

                def routing():
                    b = ri - 1
                    at = [0]

                    def step(ins):
                        at[0] += 1
                        ins.then_inc(route, 1)
                        dve.wait_ge(route, b * RD + at[0])

                    def over(x):
                        return x[:, :].unsqueeze(2).to_broadcast([P, J, E])

                    dve.wait_ge(g_mm, b + 1)
                    step(nc.vector.scalar_tensor_tensor(
                        logits[:, :, :], ps_b[:, 0:J * E].rearrange("p (j e) -> p j e", j=J), unscale[:, 3:4],
                        router_gamma[:, :].unsqueeze(1).to_broadcast([P, J, E]), ALU.mult, ALU.add))
                    step(nc.vector.tensor_reduce(top1[:, :], logits[:, :, :], AX.X, ALU.max))
                    step(nc.vector.tensor_tensor(below[:, :, :], logits[:, :, :], over(top1), ALU.subtract))
                    step(nc.vector.scalar_tensor_tensor(rank1[:, :, :], below[:, :, :], 0.0, first_wins[:, :, :],
                                                        ALU.is_equal, ALU.mult))
                    step(nc.vector.tensor_reduce(best1[:, :], rank1[:, :, :], AX.X, ALU.max))
                    step(nc.vector.tensor_tensor(pick1[:, :, :], rank1[:, :, :], over(best1), ALU.is_equal))
                    step(nc.vector.scalar_tensor_tensor(rest[:, :, :], pick1[:, :, :], MASKED, below[:, :, :],
                                                        ALU.mult, ALU.add))
                    step(nc.vector.tensor_reduce(top2[:, :], rest[:, :, :], AX.X, ALU.max))
                    step(nc.vector.tensor_tensor(tied2[:, :, :], rest[:, :, :], over(top2), ALU.is_equal))
                    step(nc.vector.tensor_tensor(rank2[:, :, :], tied2[:, :, :], first_wins[:, :, :], ALU.mult))
                    step(nc.vector.tensor_reduce(best2[:, :], rank2[:, :, :], AX.X, ALU.max))
                    step(nc.vector.tensor_tensor(pick2[:, :, :], rank2[:, :, :], over(best2), ALU.is_equal))
                    dve.wait_ge(gexp_done, b + 1)
                    nc.vector.tensor_reduce(expo_sum[:, :], expo[:, :, :], AX.X, ALU.add).then_inc(zsum_done, 1)
                    dve.wait_ge(zsum_done, b + 1)
                    nc.vector.reciprocal(expo_inv[:, :], expo_sum[:, :]).then_inc(inv_done, 1)

                def start_acc():
                    b = ri - 1
                    dve.wait_ge(b_mm, b + 1)
                    if late(i, b, 2):
                        dve.wait_ge(fin_done, (b - 1) * J)
                    nc.vector.scalar_tensor_tensor(acc[nxt][:, :, :].rearrange("p j d -> p (j d)"), ps_b[:, :],
                                                   unscale[:, 5:6], h2[nxt][:, :, :].rearrange("p j d -> p (j d)"),
                                                   ALU.mult, ALU.add).then_inc(acc_init, 1)

                def add_experts(j, back):
                    b = ri - back
                    q = par if back == 2 else nxt
                    if j == 0:
                        dve.wait_ge(acc_init, b + 1)
                        dve.wait_ge(route_p, b * RP + RP)
                    dve.wait_ge(y_even_mm, b * J + j + 1)
                    for e in range(HE):
                        nc.vector.scalar_tensor_tensor(acc[q][:, j, :], ps_y[0][:, e * D:(e + 1) * D],
                                                       combine_y[q][:, j, e:e + 1], acc[q][:, j, :],
                                                       ALU.mult, ALU.add).then_inc(acc_step, 1)
                        if e < HE - 1:
                            dve.wait_ge(acc_step, (b * J + j) * HE + e + 1)

                now, after, e1, e2 = has(i, 0), has(i, 1), has(i, -1), has(i, -2)
                if e1:
                    norm_2()
                    u2_lo()
                if e2:
                    add_experts(2, 2)
                if e1:
                    routing()
                if e2:
                    add_experts(3, 2)
                if has(i, 2):
                    one_hot()
                if after:
                    stats_1()
                if e1:
                    start_acc()
                if after:
                    norm_1()
                if now:
                    residual(0)
                if after:
                    u1_lo()
                if e1:
                    add_experts(0, 1)
                if after:
                    p_lo()
                if now:
                    residual(1)
                if e1:
                    add_experts(1, 1)

            run(dve, body)

        @block.gpsimd
        def _(pool):
            count = [0]

            def link(ins):
                count[0] += 1
                ins.then_inc(pool_setup, 1)
                pool.wait_ge(pool_setup, count[0])

            nc.gpsimd.memset(amax[:, :], 0.0).then_inc(amax_zeroed, 1)
            link(nc.gpsimd.memset(sixteenth[:, :], 1.0 / NI))
            link(nc.gpsimd.memset(ident[:, :], 0.0))
            nc.gpsimd.affine_select(out=ident[:, :], in_=ident[:, :], compare_op=ALU.not_equal, fill=1.0, base=0,
                                    pattern=[[-1, P]], channel_multiplier=1).then_inc(consts_made, 1)
            pool.wait_ge(consts_made, 1)
            link(nc.gpsimd.tensor_copy(ident16[:, :], ident[:, :]))
            link(nc.gpsimd.memset(row_expert[:, :, :], 0.0))
            link(nc.gpsimd.memset(lo_rows[:, :, :], 0.0))
            link(nc.gpsimd.memset(bias_blocks[:, :, :], 0.0))
            link(nc.gpsimd.affine_select(out=row_expert[:, :, :], in_=row_expert[:, :, :], compare_op=ALU.not_equal,
                                         fill=1.0, base=0, pattern=[[-1, E], [-E, P // E]], channel_multiplier=1))
            nc.gpsimd.affine_select(out=lo_rows[:, :, :], in_=lo_rows[:, :, :], compare_op=ALU.not_equal,
                                    fill=1.0, base=-16, pattern=[[-32, J], [-1, 16]], channel_multiplier=1)\
              .then_inc(consts_made, 1)
            pool.wait_ge(amax_found, 4)
            nc.gpsimd.partition_all_reduce(amax_all[:, :], amax[:, :], P, ABSMAX).then_inc(amax_spread, 1)
            link(nc.gpsimd.iota(vocab_id[:, :], pattern=[[0, 1]], base=0, channel_multiplier=1,
                                allow_small_or_imprecise_dtypes=True))
            link(nc.gpsimd.iota(first_wins[:, :, :], pattern=[[0, J], [-1, E]], base=E, channel_multiplier=0,
                                allow_small_or_imprecise_dtypes=True))
            link(nc.gpsimd.memset(minus_half[:, :], -0.5))
            link(nc.gpsimd.memset(eps[:, :], EPS))
            link(nc.gpsimd.memset(lift[:, :], LIFT))
            link(nc.gpsimd.memset(cpack[:, :, :], 0.0))
            for n in range(2):
                link(nc.gpsimd.memset(onehot[n][:, 0:1], 0.0))
                link(nc.gpsimd.memset(u1[n][:, :, D:D + 4], 1.0))
            pool.wait_ge(amax_found, 6)
            nc.gpsimd.partition_all_reduce(amax2_all[:, :], amax2[:, :], P, ABSMAX).then_inc(amax_spread, 1)

            def body(i, ri, par):
                nxt = 1 - par

                def rstd(mv, var, rs, mv_sem, at, var_sem, rs_sem, b):
                    pool.wait_ge(mv_sem, at)
                    nc.gpsimd.tensor_tensor(var[:, :], mv[:, :, 1], eps[:, :], ALU.add)\
                      .then_inc(var_sem, 1)
                    pool.wait_ge(var_sem, b + 1)
                    nc.gpsimd.tensor_tensor(rs[:, :], var[:, :], minus_half[:, :], ALU.pow).then_inc(rs_sem, 1)

                def combine_weights():
                    b = ri - 1
                    at = [0]

                    def step(ins):
                        at[0] += 1
                        ins.then_inc(route_p, 1)
                        pool.wait_ge(route_p, b * RP + at[0])

                    def over(x):
                        return x.unsqueeze(2).to_broadcast([P, J, E])

                    pool.wait_ge(route, b * RD + 12)
                    step(nc.gpsimd.tensor_tensor(picks[:, :, :], pick1[:, :, :], pick2[:, :, :], ALU.add))
                    pool.wait_ge(gexp_done, b + 1)
                    step(nc.gpsimd.tensor_tensor(picked[:, :, :], picks[:, :, :], expo[:, :, :], ALU.mult))
                    pool.wait_ge(inv_done, b + 1)
                    step(nc.gpsimd.tensor_tensor(inv_lift[:, :], expo_inv[:, :], lift[:, :], ALU.mult))
                    step(nc.gpsimd.tensor_tensor(combine[:, :, :], picked[:, :, :], over(inv_lift[:, :]), ALU.mult))
                    if late(i, b):
                        pool.wait_ge(ct_mm, b)
                    for at_hi in (0, 2 * E):
                        step(nc.gpsimd.tensor_tensor(cpack[:, :, at_hi:at_hi + E], picked[:, :, :],
                                                     over(inv_lift[:, :]), ALU.mult))
                    step(nc.gpsimd.tensor_tensor(cpack[:, :, E:2 * E], combine[:, :, :], cpack[:, :, 0:E],
                                                 ALU.subtract))
                    if late(i, b, 2):
                        pool.wait_ge(acc_step, (b - 1) * J * HE)
                    step(nc.gpsimd.tensor_tensor(combine_y[nxt][:, :, :], combine[:, :, :],
                                                 unscale[:, 4:5].unsqueeze(2).to_broadcast([P, J, E]), ALU.mult))

                def sum_odd(j, back):
                    b = ri - back
                    q = par if back == 2 else nxt
                    at = (b * J + j) * 3
                    pool.wait_ge(y_odd_done, b * J + j + 1)
                    nc.gpsimd.tensor_tensor(prod[:, :, :], y_odd[j % 2][:, :, :],
                                            combine_y[q][:, j, HE:E].unsqueeze(2).to_broadcast([P, HE, D]),
                                            ALU.mult).then_inc(y_sum, 1)
                    pool.wait_ge(y_sum, at + 1)
                    nc.gpsimd.tensor_tensor(sum2[:, :, :], prod[:, 0:2, :], prod[:, 2:4, :], ALU.add).then_inc(y_sum, 1)
                    pool.wait_ge(y_sum, at + 2)
                    nc.gpsimd.tensor_tensor(sum1[:, :], sum2[:, 0, :], sum2[:, 1, :], ALU.add).then_inc(y_sum, 1)
                    pool.wait_ge(y_sum, at + 3)
                    pool.wait_ge(acc_step, (b * J + j + 1) * HE)
                    if j == 0 and late(i, b, 2):
                        pool.wait_ge(out_stored[q], 8 * (b - q))
                    nc.gpsimd.tensor_tensor(out_sb[q][:, j, :], acc[q][:, j, :], sum1[:, :], ALU.add)\
                      .then_inc(fin_done, 1)

                now, after, e1, e2 = has(i, 0), has(i, 1), has(i, -1), has(i, -2)
                if e1:
                    rstd(mv2, var2, rstd2, mv2_done, (ri - 1) * 2 + 2, var2_done, rstd2_done, ri - 1)
                if e2:
                    sum_odd(1, 2)
                if e2:
                    sum_odd(2, 2)
                if e1:
                    combine_weights()
                if after:
                    rstd(mv1, var1, rstd1, mv1_done, ri + 2, var1_done, rstd1_done, ri + 1)
                if e2:
                    sum_odd(3, 2)
                if e1:
                    sum_odd(0, 1)

            pool.wait_ge(weights_ready, 1)
            run(pool, body)


_INS = ['x', 'L0_tok_emb_weight', 'L0_tok_conv_weight', 'L0_attn_attention_weights', 'L0_ffn_Ins_tk',
        'L0_ffn_gate_w', 'L0_ffn_expert_w', 'L0_ffn_expert_b', 'L0_ffn_gamma_w', 'L0_ffn_beta_w', 'L0_ffn_rmod_w']


def kernel(**inputs):
    import numpy as _np
    import concourse.bacc as _bacc
    from concourse import mybir as _mybir
    from concourse.bass_utils import run_bass_kernel_spmd as _run

    nc = _bacc.Bacc("TRN2", target_bir_lowering=False, num_devices=1)
    arrays, args = {}, []
    for name in _INS:
        a = _np.ascontiguousarray(inputs[name])
        arrays[f"in_{name}_dram"] = a
        args.append(nc.dram_tensor(f"in_{name}_dram", a.shape, _mybir.dt.from_np(a.dtype), kind="ExternalInput").ap())
    batch, seq = inputs['x'].shape
    width = inputs['L0_tok_emb_weight'].shape[1]
    args.append(nc.dram_tensor("out_dram", (batch, seq, width), _mybir.dt.float32, kind="ExternalOutput").ap())
    tower_kernel(nc, *args)
    r = _run(nc, [arrays], core_ids=[0])
    return r.results[0]["out_dram"]
```

```python
import concourse.bass as bass
from concourse import mybir
from contextlib import ExitStack


def tower_kernel(
    nc: bass.Bass,
    tokens: bass.AP,
    emb_weight: bass.AP,
    conv_weight: bass.AP,
    attn_weight: bass.AP,
    instructions: bass.AP,
    gate_weight: bass.AP,
    expert_weight: bass.AP,
    expert_bias: bass.AP,
    gamma_weight: bass.AP,
    beta_weight: bass.AP,
    rmod_weight: bass.AP,
    out: bass.AP,
):
    fp32 = mybir.dt.float32
    fp16 = mybir.dt.float16
    i32 = mybir.dt.int32
    ALU = mybir.AluOpType
    ACT = mybir.ActivationFunctionType
    AX = mybir.AxisListType
    ABSMAX = bass.bass_isa.ReduceOp.absmax

    B, S = tokens.shape
    V, D = emb_weight.shape
    E = gate_weight.shape[1]
    NI = instructions.shape[1]
    P = 128
    J = S // P
    HE = E // 2
    EPS = 1e-5
    QMAX = 127.0
    ROUND = 12582912.0
    LIFT = 1024.0
    TINY = 1e-30
    EXPONENT_BITS = 0x7F800000
    PROJ_SCALE = 2.0 ** -14
    MASKED = -1e30

    y_rows = tokens
    out_rows = out.rearrange("b (p j) d -> b p j d", j=J)

    ctx = ExitStack()
    with ctx:
        def sb(name, shape, dt):
            return ctx.enter_context(nc.sbuf_tensor(name, shape, dt))

        def sem(name):
            return ctx.enter_context(nc.semaphore(name))

        emb = sb("emb", [P, D], fp32)
        conv = sb("conv", [P, D * 2], fp32)
        conv_q = sb("conv_q", [P, D * 2], fp32)
        emb_q = sb("emb_q", [P, D], fp32)
        table = sb("table", [P, 2, D], fp32)
        table_hi = sb("table_hi", [P, 2, D], fp16)
        table_lo = sb("table_lo", [P, 2, D], fp16)
        attn_w = sb("attn_w", [P, D], fp32)
        attn_hi = sb("attn_hi", [P, D], fp16)
        attn_lo = sb("attn_lo", [P, D], fp16)
        gate_w = sb("gate_w", [P, E], fp32)
        gate_hi = sb("gate_hi", [P, E], fp16)
        gate_lo = sb("gate_lo", [P, E], fp16)
        expert_w = sb("expert_w", [P, E, D], fp32)
        expert_hi = sb("expert_hi", [P, E, D], fp16)
        expert_lo = sb("expert_lo", [P, E, D], fp16)
        expert_b = sb("expert_b", [P, E, D], fp32)
        beta_w = sb("beta_w", [P, E, D], fp32)
        bias_all = sb("bias_all", [P, E, D], fp32)
        gamma_w = sb("gamma_w", [E, D], fp32)
        gamma_t = sb("gamma_t", [P, E], fp32)
        rmod_w = sb("rmod_w", [P, E], fp32)
        ins_w = sb("ins_w", [NI, D], fp32)
        ins_mean = sb("ins_mean", [P, P], fp32)
        sixteenth = sb("sixteenth", [NI, P], fp32)
        router_gamma = sb("router_gamma", [P, E], fp32)
        gam = sb("gam", [P, E], fp32)
        bias_row = sb("bias_row", [P, D], fp32)
        bias_hi = sb("bias_hi", [P, D], fp16)
        bias_lo = sb("bias_lo", [P, D], fp16)
        bias_blocks = sb("bias_blocks", [P, J, D], fp16)
        row_expert = sb("row_expert", [P, E, P // E], fp32)
        row_is = sb("row_is", [P, E], fp32)
        lo_rows = sb("lo_rows", [P, J, 16], fp32)
        is_lo = sb("is_lo", [P, 1], fp32)
        is_hi = sb("is_hi", [P, 1], fp32)
        amax = sb("amax", [P, 4], fp32)
        amax_all = sb("amax_all", [P, 4], fp32)
        amax2 = sb("amax2", [P, 2], fp32)
        amax2_all = sb("amax2_all", [P, 2], fp32)
        step_of = sb("step_of", [P, 6], fp32)
        inv_step = sb("inv_step", [P, 6], fp32)
        unscale = sb("unscale", [P, 6], fp32)
        h_scale = sb("h_scale", [P, 1], fp32)
        vocab_id = sb("vocab_id", [P, 1], fp32)
        first_wins = sb("first_wins", [P, J, E], fp32)
        minus_half = sb("minus_half", [P, J], fp32)
        idle = sb("idle", [P, 3], fp32)
        eps = sb("eps", [P, J], fp32)
        lift = sb("lift", [P, J], fp32)
        ident = sb("ident", [P, P], fp32)
        ident16 = sb("ident16", [P, P], fp16)

        y_bc = [sb(f"y_bc{n}", [P, S], i32) for n in range(2)]
        onehot = [sb(f"onehot{n}", [P, S + 1], fp16) for n in range(2)]
        h1 = [sb(f"h1_{n}", [P, J, D], fp32) for n in range(4)]
        u1 = [sb(f"u1_{n}", [P, J, D + 4], fp32) for n in range(4)]
        shift1 = sb("shift1", [P, J], fp32)
        stats1 = sb("stats1", [P, J, 6], fp32)
        mv1 = sb("mv1", [P, J, 2], fp32)
        var1 = sb("var1", [P, J], fp32)
        rstd1 = sb("rstd1", [P, J], fp32)
        uT_hi = sb("uT_hi", [P, S], fp16)
        uT_lo = sb("uT_lo", [P, S], fp16)
        pT_hi = sb("pT_hi", [P, S], fp16)
        pT_lo = sb("pT_lo", [P, S], fp16)
        th = [sb(f"th{n}", [P, S], fp32) for n in range(2)]
        probs = sb("probs", [P, J, S], fp32)
        inv_z = sb("inv_z", [P, 2, 2], fp32)
        h2 = [sb(f"h2_{n}", [P, J, D], fp32) for n in range(2)]
        stats2 = sb("stats2", [P, J, 6], fp32)
        mv2 = sb("mv2", [P, J, 2], fp32)
        var2 = sb("var2", [P, J], fp32)
        rstd2 = sb("rstd2", [P, J], fp32)
        u2 = sb("u2", [P, J, D], fp32)
        u2T_hi = [sb(f"u2T_hi{n}", [P, S], fp16) for n in range(2)]
        u2T_lo = [sb(f"u2T_lo{n}", [P, S], fp16) for n in range(2)]
        logits = sb("logits", [P, J, E], fp32)
        top1 = sb("top1", [P, J], fp32)
        below = sb("below", [P, J, E], fp32)
        expo = sb("expo", [P, J, E], fp32)
        expo_sum = sb("expo_sum", [P, J], fp32)
        expo_inv = sb("expo_inv", [P, J], fp32)
        inv_lift = sb("inv_lift", [P, J], fp32)
        rank1 = sb("rank1", [P, J, E], fp32)
        best1 = sb("best1", [P, J], fp32)
        pick1 = sb("pick1", [P, J, E], fp32)
        rest = sb("rest", [P, J, E], fp32)
        top2 = sb("top2", [P, J], fp32)
        tied2 = sb("tied2", [P, J, E], fp32)
        rank2 = sb("rank2", [P, J, E], fp32)
        best2 = sb("best2", [P, J], fp32)
        pick2 = sb("pick2", [P, J, E], fp32)
        picks = sb("picks", [P, J, E], fp32)
        picked = sb("picked", [P, J, E], fp32)
        combine = sb("combine", [P, J, E], fp32)
        combine_y = [sb(f"combine_y{n}", [P, J, E], fp32) for n in range(2)]
        cpack = sb("cpack", [P, J, 32], fp16)
        cT = sb("cT", [P, P], fp16)
        acc = [sb(f"acc{n}", [P, J, D], fp32) for n in range(2)]
        y_odd = [sb(f"y_odd{n}", [P, HE, D], fp32) for n in range(2)]
        sum2 = [sb(f"sum2_{n}", [P, 2, D], fp32) for n in range(2)]
        sum1 = [sb(f"sum1_{n}", [P, D], fp32) for n in range(2)]
        out_sb = [sb(f"out_sb{n}", [P, J, D], fp32) for n in range(2)]

        def bank(name):
            return ctx.enter_context(nc.psum_tensor(name, [P, 512], fp32))

        ps_s = [bank(f"ps_s{n}") for n in range(2)]
        ps_y = [bank(f"ps_y{n}") for n in range(2)]
        ps_o = [bank(f"ps_o{n}") for n in range(2)]
        ps_a = bank("ps_a")
        ps_b = bank("ps_b")
        O_STEP = 256

        loaded = {n: sem(f"loaded_{n}") for n in ("emb", "conv", "attn", "gate", "expert", "bias", "beta", "small")}
        amax_zeroed = sem("amax_zeroed")
        consts_made = sem("consts_made")
        amax_spread = sem("amax_spread")
        pool_setup = sem("pool_setup")
        dve_setup = sem("dve_setup")
        amax_found = sem("amax_found")
        means_out = sem("means_out")
        means_mm = sem("means_mm")
        weights_ready = sem("weights_ready")
        y_loaded = [sem(f"y_loaded{n}") for n in range(2)]
        out_stored = [sem(f"out_stored{n}") for n in range(2)]
        onehot_ready = sem("onehot_ready")
        h_mm = sem("h_mm")
        h_relu = sem("h_relu")
        st1_done = sem("st1_done")
        mv1_done = sem("mv1_done")
        var1_done = sem("var1_done")
        rstd1_done = sem("rstd1_done")
        shift1_done = sem("shift1_done")
        u1_done = sem("u1_done")
        t_mm = sem("t_mm")
        uthi_done = sem("uthi_done")
        utlo_done = sem("utlo_done")
        p_mm = sem("p_mm")
        phi_done = sem("phi_done")
        plo_done = sem("plo_done")
        s_mm = sem("s_mm")
        tanh_done = sem("tanh_done")
        exp_done = sem("exp_done")
        o_mm = sem("o_mm")
        invz_done = sem("invz_done")
        h2_done = sem("h2_done")
        st2_done = sem("st2_done")
        mv2_done = sem("mv2_done")
        var2_done = sem("var2_done")
        rstd2_done = sem("rstd2_done")
        u2_done = sem("u2_done")
        u2_mm = sem("u2_mm")
        u2hi_done = sem("u2hi_done")
        u2lo_done = sem("u2lo_done")
        g_mm = sem("g_mm")
        route = sem("route")
        gexp_done = sem("gexp_done")
        route_p = sem("route_p")
        zsum_done = sem("zsum_done")
        inv_done = sem("inv_done")
        ct_mm = sem("ct_mm")
        ct_done = sem("ct_done")
        b_mm = sem("b_mm")
        acc_init = sem("acc_init")
        y_even_mm = sem("y_even_mm")
        y_odd_mm = sem("y_odd_mm")
        acc_step = sem("acc_step")
        y_odd_done = sem("y_odd_done")
        y_sum = sem("y_sum")
        fin_done = sem("fin_done")

        RD = 12
        RP = 7
        RP_PACKED = 6

        UNROLL = 4
        LOOP_FROM, LOOP_TO = 8, 28
        FIRST_ROUND, END_ROUND = -4, B + 4

        def run(eng, body):
            for r in range(FIRST_ROUND, LOOP_FROM):
                body(r, r, r % UNROLL)
            with eng.Fori(LOOP_FROM // UNROLL, LOOP_TO // UNROLL) as turn:
                for k in range(UNROLL):
                    body(None, turn * UNROLL + k, k)
            for r in range(LOOP_TO, END_ROUND):
                body(r, r, r % UNROLL)

        def has(i, n):
            return i is None or 0 <= i + n < B

        def late(i, b, n=1):
            return i is None or b >= n

        block = ctx.enter_context(nc.Block())

        @block.sync
        def _(sp):
            sp.dma_start(emb[0:V, :], emb_weight).then_inc(loaded["emb"], 16)
            sp.dma_start(conv[:, :], conv_weight.rearrange("d o k -> (d o k)").partition_broadcast(P))\
              .then_inc(loaded["conv"], 16)
            sp.dma_start(y_bc[0][0:V, :], y_rows[0, :].partition_broadcast(V)).then_inc(y_loaded[0], 16)
            sp.dma_start(y_bc[1][0:V, :], y_rows[1, :].partition_broadcast(V)).then_inc(y_loaded[1], 16)
            sp.dma_start(attn_w[:, :], attn_weight).then_inc(loaded["attn"], 16)
            sp.dma_start(ins_w[:, :], instructions[0, :, :]).then_inc(loaded["small"], 16)
            sp.dma_start(gamma_w[:, :], gamma_weight).then_inc(loaded["small"], 16)
            sp.dma_start(rmod_w[:, :], rmod_weight).then_inc(loaded["small"], 16)
            sp.dma_start(gate_w[:, :], gate_weight).then_inc(loaded["gate"], 16)
            sp.dma_start(expert_w[:, :, :], expert_weight.rearrange("e l d -> l e d")).then_inc(loaded["expert"], 16)
            sp.dma_start(beta_w[:, :, :], beta_weight.rearrange("e h d -> h e d")).then_inc(loaded["beta"], 16)
            sp.dma_start(expert_b[:, :, :].rearrange("p e d -> p (e d)"),
                         expert_bias.rearrange("e d -> (e d)").partition_broadcast(P)).then_inc(loaded["bias"], 16)

            def body(i, r, k):
                if has(i, 4) and late(i, r + 4, 2):
                    sp.wait_ge(onehot_ready, r + 3)
                    sp.dma_start(y_bc[k % 2][0:V, :], y_rows[r + 4, :].partition_broadcast(V))\
                      .then_inc(y_loaded[k % 2], 16)
                if has(i, -3):
                    sp.wait_ge(fin_done, (r - 3) * J + J)
                    sp.dma_start(out_rows[r - 3, :, :, :], out_sb[(k + 3) % 2][:, :, :])\
                      .then_inc(out_stored[(k + 3) % 2], 16)

            run(sp, body)
            for n in range(2):
                sp.wait_ge(out_stored[n], 16 * (B // 2))

        @block.tensor
        def _(pe):
            pe.wait_ge(loaded["small"], 48)
            pe.wait_ge(consts_made, 1)
            nc.tensor.matmul(ps_a[:, 0:P], ins_w[:, :], sixteenth[:, :], start=True, stop=True).then_inc(means_mm, 1)
            nc.tensor.transpose(ps_b[:, 0:E], gamma_w[:, :], ident[0:E, 0:E]).then_inc(means_mm, 1)
            pe.wait_ge(means_out, 2)
            nc.tensor.matmul(ps_a[:, 0:E], ins_mean[:, :], rmod_w[:, :], start=True, stop=True)
            nc.tensor.matmul(ps_a[:, E:2 * E], ins_mean[:, :], gamma_t[:, :], start=True, stop=True).then_inc(means_mm, 1)
            pe.wait_ge(loaded["beta"], 16)
            for n in range(2):
                nc.tensor.matmul(ps_y[n][:, :], ins_mean[:, :], beta_w[:, n * HE:(n + 1) * HE, :],
                                 start=True, stop=True).then_inc(means_mm, 1)

            def body(i, r, k):
                def scores(b, q, t):
                    if t == 0:
                        pe.wait_ge(plo_done, b + 1)
                    if t >= 2 or late(i, b):
                        pe.wait_ge(tanh_done, b * J + t - 1)
                    for n, (a, c) in enumerate(((uT_hi, pT_hi), (uT_hi, pT_lo), (uT_lo, pT_hi))):
                        last = nc.tensor.matmul(ps_s[t % 2][:, :], a[:, t * P:(t + 1) * P], c[:, :],
                                                start=(n == 0), stop=(n == 2))
                    last.then_inc(s_mm, 1)

                def attend(b, q, s):
                    if s == 0:
                        pe.wait_ge(exp_done, b * J + J)
                    if s % 2 == 0 and late(i, b):
                        pe.wait_ge(h2_done, b * 2 - 1 + s // 2)
                    o = ps_o[s // 2][:, (s % 2) * O_STEP:(s % 2) * O_STEP + D + 1]
                    for t in range(J):
                        last = nc.tensor.matmul(o, probs[:, t, s * P:(s + 1) * P], u1[q][:, t, 0:D + 1],
                                                start=(t == 0), stop=(t == J - 1))
                    if s % 2:
                        last.then_inc(o_mm, 1)

                def embed(b, q):
                    pe.wait_ge(onehot_ready, b + 1)
                    if late(i, b, 2):
                        pe.wait_ge(plo_done, b - 1)
                    elif b == 1:
                        pe.wait_ge(h_relu, 1)
                    for j in range(J):
                        n = 0
                        for tap in range(2):
                            toks = onehot[q % 2][0:V, tap + j:tap + j + J * (P - 1) + 1:J]
                            for part in (table_hi, table_lo):
                                last = nc.tensor.matmul(ps_a[:, j * D:(j + 1) * D], toks, part[0:V, tap, :],
                                                        start=(n == 0), stop=(n == 3))
                                n += 1
                    last.then_inc(h_mm, 1)

                def turn_u1(b, q):
                    pe.wait_ge(u1_done, b + 1)
                    if i is None or b + 1 < B:
                        pe.wait_ge(h_relu, b + 2)
                    for j in range(J):
                        last = nc.tensor.transpose(ps_a[:, j * P:(j + 1) * P], u1[q][:, j, 0:D], ident[:, :])
                    last.then_inc(t_mm, 1)

                def project(b, q):
                    pe.wait_ge(utlo_done, b + 1)
                    for n, (a, c) in enumerate(((attn_hi, uT_hi), (attn_hi, uT_lo), (attn_lo, uT_hi))):
                        last = nc.tensor.matmul(ps_a[:, :], a[:, :], c[:, :], start=(n == 0), stop=(n == 2))
                    last.then_inc(p_mm, 1)

                def turn_u2(b, q):
                    pe.wait_ge(u2_done, b + 1)
                    if late(i, b):
                        pe.wait_ge(acc_init, b)
                    for j in range(J):
                        last = nc.tensor.transpose(ps_b[:, j * P:(j + 1) * P], u2[:, j, :], ident[:, :])
                    last.then_inc(u2_mm, 1)

                def gate(b, q):
                    pe.wait_ge(u2lo_done, b + 1)
                    for j in range(J):
                        rows = slice(j * P, (j + 1) * P)
                        for n, (a, c) in enumerate(((u2T_hi, gate_hi), (u2T_hi, gate_lo), (u2T_lo, gate_hi))):
                            last = nc.tensor.matmul(ps_b[:, j * E:(j + 1) * E], a[q % 2][:, rows], c[:, :],
                                                    start=(n == 0), stop=(n == 2))
                    last.then_inc(g_mm, 1)

                def turn_combine(b, q):
                    pe.wait_ge(route_p, b * RP + RP_PACKED)
                    nc.tensor.transpose(ps_b[:, 0:P // 2].bitcast(fp16), cpack[:, :, :].rearrange("p j c -> p (j c)"),
                                        ident16[:, :]).then_inc(ct_mm, 1)

                def bias_rows(b, q):
                    pe.wait_ge(ct_done, b + 1)
                    nc.tensor.matmul(ps_b[:, :], cT[:, :], bias_blocks[:, :, :], start=True, stop=True)\
                      .then_inc(b_mm, 1)

                def experts(b, q, j, half):
                    if j > 0 or late(i, b):
                        if half:
                            pe.wait_ge(y_odd_done, b * J + j)
                        else:
                            pe.wait_ge(acc_step, (b * J + j) * HE)
                    rows = slice(j * P, (j + 1) * P)
                    es = slice(half * HE, (half + 1) * HE)
                    for n, (a, c) in enumerate(((u2T_hi, expert_hi), (u2T_hi, expert_lo), (u2T_lo, expert_hi))):
                        last = nc.tensor.matmul(ps_y[half][:, :], a[q % 2][:, rows], c[:, es, :],
                                                start=(n == 0), stop=(n == 2))
                    last.then_inc(y_odd_mm if half else y_even_mm, 1)

                now, in1, in2, in3, in4 = (has(i, n) for n in range(5))
                ago1, ago2, ago3, ago4 = (has(i, -n) for n in range(1, 5))
                if now:
                    turn_u1(r, k)
                if ago2:
                    turn_u2(r - 2, (k + 2) % 4)
                if ago1:
                    attend(r - 1, (k + 3) % 4, 0)
                if ago3:
                    experts(r - 3, (k + 1) % 4, 1, 1)
                    experts(r - 3, (k + 1) % 4, 1, 0)
                if ago2:
                    gate(r - 2, (k + 2) % 4)
                if ago1:
                    attend(r - 1, (k + 3) % 4, 1)
                if ago3:
                    experts(r - 3, (k + 1) % 4, 2, 1)
                if now:
                    project(r, k)
                if ago1:
                    attend(r - 1, (k + 3) % 4, 2)
                if ago3:
                    experts(r - 3, (k + 1) % 4, 2, 0)
                if ago1:
                    attend(r - 1, (k + 3) % 4, 3)
                if ago3:
                    experts(r - 3, (k + 1) % 4, 3, 1)
                if now:
                    scores(r, k, 0)
                    scores(r, k, 1)
                if ago3:
                    experts(r - 3, (k + 1) % 4, 3, 0)
                if in2:
                    embed(r + 2, (k + 2) % 4)
                if now:
                    scores(r, k, 2)
                if ago2:
                    turn_combine(r - 2, (k + 2) % 4)
                if now:
                    scores(r, k, 3)
                if ago2:
                    experts(r - 2, (k + 2) % 4, 0, 1)
                    bias_rows(r - 2, (k + 2) % 4)
                    experts(r - 2, (k + 2) % 4, 0, 0)

            pe.wait_ge(weights_ready, 1)
            run(pe, body)

        @block.scalar
        def _(act):
            act.wait_ge(means_mm, 1)
            nc.scalar.activation(ins_mean[:, :], ps_a[:, 0:P], ACT.Copy).then_inc(means_out, 1)
            act.wait_ge(means_mm, 2)
            nc.scalar.activation(gamma_t[:, :], ps_b[:, 0:E], ACT.Copy).then_inc(means_out, 1)
            act.wait_ge(weights_ready, 1)

            def body(i, r, k):
                def tanh(b, q, t):
                    act.wait_ge(s_mm, b * J + t + 1)
                    if t >= 2 or late(i, b):
                        act.wait_ge(exp_done, b * J + t - 1)
                    nc.scalar.activation(th[t % 2][:, :], ps_s[t % 2][:, :], ACT.Tanh, scale=unscale[:, 2:3])\
                      .then_inc(tanh_done, 1)

                def exp(b, q, t):
                    act.wait_ge(tanh_done, b * J + t + 1)
                    if t == 0 and late(i, b):
                        act.wait_ge(o_mm, b * 2)
                    nc.scalar.activation(probs[:, t, :], th[t % 2][:, :], ACT.Exp).then_inc(exp_done, 1)

                def relu(b, q):
                    act.wait_ge(h_mm, b + 1)
                    if late(i, b, 4):
                        act.wait_ge(h2_done, (b - 4) * 2 + 2)
                    nc.scalar.activation(h1[q][:, :, :], ps_a[:, :].rearrange("p (j d) -> p j d", j=J), ACT.Relu,
                                         scale=h_scale[:, 0:1]).then_inc(h_relu, 1)

                def norm_1(b, q):
                    act.wait_ge(shift1_done, b + 1)
                    if late(i, b, 4):
                        act.wait_ge(o_mm, (b - 4) * 2 + 2)
                    for j in range(J):
                        last = nc.scalar.activation(u1[q][:, j, 0:D], h1[q][:, j, :], ACT.Identity,
                                                    bias=shift1[:, j:j + 1], scale=rstd1[:, j:j + 1])
                    last.then_inc(u1_done, 1)

                def u1_hi(b, q):
                    act.wait_ge(t_mm, b + 1)
                    if late(i, b):
                        act.wait_ge(s_mm, b * J)
                    nc.scalar.activation(uT_hi[:, :], ps_a[:, :], ACT.Copy, scale=LIFT).then_inc(uthi_done, 1)

                def p_hi(b, q):
                    act.wait_ge(p_mm, b + 1)
                    nc.scalar.activation(pT_hi[:, :], ps_a[:, :], ACT.Copy, scale=PROJ_SCALE).then_inc(phi_done, 1)

                def u2_hi(b, q):
                    act.wait_ge(u2_mm, b + 1)
                    if late(i, b, 2):
                        act.wait_ge(y_even_mm, (b - 1) * J)
                    nc.scalar.activation(u2T_hi[q % 2][:, :], ps_b[:, :], ACT.Copy, scale=LIFT).then_inc(u2hi_done, 1)

                def gate_exp(b, q):
                    act.wait_ge(route, b * RD + 3)
                    nc.scalar.activation(expo[:, :, :], below[:, :, :], ACT.Exp).then_inc(gexp_done, 1)

                def c_out(b, q):
                    act.wait_ge(ct_mm, b + 1)
                    if late(i, b):
                        act.wait_ge(b_mm, b)
                    nc.scalar.activation(cT[:, :], ps_b[:, 0:P // 2].bitcast(fp16), ACT.Copy).then_inc(ct_done, 1)

                def y_out(b, q, j):
                    act.wait_ge(y_odd_mm, b * J + j + 1)
                    if j == 0:
                        act.wait_ge(route_p, b * RP + RP)
                    if j >= 2 or late(i, b):
                        act.wait_ge(y_sum, (b * J + j - 1) * 2 - 1)
                    for e in range(HE):
                        last = nc.scalar.activation(y_odd[j % 2][:, e, :], ps_y[1][:, e * D:(e + 1) * D], ACT.Copy,
                                                    scale=combine_y[q % 2][:, j, HE + e:HE + e + 1])
                    last.then_inc(y_odd_done, 1)

                now, in1, in2, in3, in4 = (has(i, n) for n in range(5))
                ago1, ago2, ago3, ago4 = (has(i, -n) for n in range(1, 5))
                if ago3:
                    y_out(r - 3, (k + 1) % 4, 0)
                if ago2:
                    u2_hi(r - 2, (k + 2) % 4)
                if now:
                    u1_hi(r, k)
                if ago3:
                    y_out(r - 3, (k + 1) % 4, 1)
                if ago2:
                    gate_exp(r - 2, (k + 2) % 4)
                if now:
                    p_hi(r, k)
                if ago3:
                    y_out(r - 3, (k + 1) % 4, 2)
                if in1:
                    norm_1(r + 1, (k + 1) % 4)
                if ago3:
                    y_out(r - 3, (k + 1) % 4, 3)
                if now:
                    tanh(r, k, 0)
                    tanh(r, k, 1)
                    exp(r, k, 0)
                    exp(r, k, 1)
                if in2:
                    relu(r + 2, (k + 2) % 4)
                if ago2:
                    c_out(r - 2, (k + 2) % 4)
                if now:
                    tanh(r, k, 2)
                    tanh(r, k, 3)
                    exp(r, k, 2)
                    exp(r, k, 3)

            run(act, body)

        @block.vector
        def _(dve):
            count = [0]

            def link(ins):
                count[0] += 1
                ins.then_inc(dve_setup, 1)
                dve.wait_ge(dve_setup, count[0])

            for n, (name, ap) in enumerate((("emb", emb[0:V, :]), ("conv", conv[:, :]), ("attn", attn_w[:, :]),
                                            ("gate", gate_w[:, :]))):
                if n == 0:
                    dve.wait_ge(amax_zeroed, 1)
                dve.wait_ge(loaded[name], 16)
                nc.vector.tensor_reduce(amax[0:ap.shape[0], n:n + 1], ap, AX.X, ALU.max,
                                        apply_absolute_value=True).then_inc(amax_found, 1)
            dve.wait_ge(amax_spread, 1)
            link(nc.vector.tensor_scalar(step_of[:, 0:2], amax_all[:, 0:2], 1.0 / QMAX, None, ALU.mult))
            link(nc.vector.reciprocal(inv_step[:, 0:2], step_of[:, 0:2]))
            link(nc.vector.tensor_tensor(h_scale[:, :], step_of[:, 0:1], step_of[:, 1:2], ALU.mult))
            link(nc.vector.tensor_scalar(conv_q[:, :], conv[:, :], inv_step[:, 1:2], ROUND, ALU.mult, ALU.add))
            link(nc.vector.tensor_scalar(conv_q[:, :], conv_q[:, :], ROUND, None, ALU.subtract))
            link(nc.vector.tensor_scalar(emb_q[0:V, :], emb[0:V, :], inv_step[0:V, 0:1], ROUND, ALU.mult, ALU.add))
            taps = conv_q[:, :].rearrange("p (d k) -> p k d", k=2)
            for k in range(2):
                link(nc.vector.scalar_tensor_tensor(table[0:V, k, :], emb_q[0:V, :], ROUND, taps[0:V, k, :],
                                                    ALU.subtract, ALU.mult))
            link(nc.vector.tensor_copy(table_hi[0:V, :, :], table[0:V, :, :]))
            link(nc.vector.tensor_tensor(table_lo[0:V, :, :], table[0:V, :, :], table_hi[0:V, :, :], ALU.subtract))

            def power(src, n):
                w = src.shape[1]
                link(nc.vector.tensor_scalar(step_of[:, n:n + w], src, TINY, None, ALU.max))
                link(nc.vector.tensor_scalar(step_of[:, n:n + w].bitcast(i32), step_of[:, n:n + w].bitcast(i32),
                                             EXPONENT_BITS, None, ALU.bitwise_and))
                link(nc.vector.reciprocal(inv_step[:, n:n + w], step_of[:, n:n + w]))
                link(nc.vector.tensor_scalar(inv_step[:, n:n + w], inv_step[:, n:n + w], LIFT, None, ALU.mult))

            def split(hi, lo, ap, scale):
                link(nc.vector.tensor_scalar(ap, ap, scale, None, ALU.mult))
                link(nc.vector.tensor_copy(hi, ap))
                link(nc.vector.tensor_tensor(lo, ap, hi, ALU.subtract))

            power(amax_all[:, 2:4], 2)
            link(nc.vector.tensor_scalar(unscale[:, 2:3], step_of[:, 2:3], 1.0 / (LIFT * LIFT * LIFT * PROJ_SCALE),
                                         None, ALU.mult))
            link(nc.vector.tensor_scalar(unscale[:, 3:4], step_of[:, 3:4], 1.0 / (LIFT * LIFT), None, ALU.mult))
            split(attn_hi[:, :], attn_lo[:, :], attn_w[:, :], inv_step[:, 2:3])
            split(gate_hi[:, :], gate_lo[:, :], gate_w[:, :], inv_step[:, 3:4])
            dve.wait_ge(means_mm, 3)
            link(nc.vector.tensor_copy(router_gamma[:, :], ps_a[:, 0:E]))
            link(nc.vector.tensor_copy(gam[:, :], ps_a[:, E:2 * E]))
            dve.wait_ge(loaded["expert"], 16)
            dve.wait_ge(loaded["bias"], 16)
            for e in range(E):
                link(nc.vector.tensor_scalar(expert_w[:, e, :], expert_w[:, e, :], gam[:, e:e + 1], None, ALU.mult))
            dve.wait_ge(means_mm, 5)
            for e in range(E):
                link(nc.vector.scalar_tensor_tensor(bias_all[:, e, :], expert_b[:, e, :], gam[:, e:e + 1],
                                                    ps_y[e // HE][:, (e % HE) * D:(e % HE + 1) * D],
                                                    ALU.mult, ALU.add))
            dve.wait_ge(consts_made, 2)
            link(nc.vector.tensor_reduce(row_is[:, :], row_expert[:, :, :], AX.X, ALU.max))
            link(nc.vector.tensor_reduce(is_lo[:, :], lo_rows[:, :, :], AX.XY, ALU.max))
            link(nc.vector.tensor_scalar(is_hi[:, :], is_lo[:, :], -1.0, 1.0, ALU.mult, ALU.add))
            link(nc.vector.tensor_scalar(bias_row[:, :], bias_all[:, 0, :], row_is[:, 0:1], None, ALU.mult))
            for e in range(1, E):
                link(nc.vector.scalar_tensor_tensor(bias_row[:, :], bias_all[:, e, :], row_is[:, e:e + 1],
                                                    bias_row[:, :], ALU.mult, ALU.add))
            nc.vector.tensor_reduce(amax2[:, 0:1], expert_w[:, :, :], AX.XY, ALU.max,
                                    apply_absolute_value=True).then_inc(amax_found, 1)
            nc.vector.tensor_reduce(amax2[:, 1:2], bias_row[:, :], AX.X, ALU.max,
                                    apply_absolute_value=True).then_inc(amax_found, 1)
            dve.wait_ge(amax_spread, 2)
            power(amax2_all[:, :], 4)
            link(nc.vector.tensor_scalar(unscale[:, 4:5], step_of[:, 4:5], 1.0 / (LIFT * LIFT * LIFT), None, ALU.mult))
            link(nc.vector.tensor_scalar(unscale[:, 5:6], step_of[:, 5:6], 1.0 / (LIFT * LIFT), None, ALU.mult))
            split(expert_hi[:, :, :], expert_lo[:, :, :], expert_w[:, :, :], inv_step[:, 4:5])
            split(bias_hi[:, :], bias_lo[:, :], bias_row[:, :], inv_step[:, 5:6])
            link(nc.vector.tensor_scalar(bias_hi[:, :], bias_hi[:, :], is_hi[:, 0:1], None, ALU.mult))
            link(nc.vector.scalar_tensor_tensor(bias_hi[:, :], bias_lo[:, :], is_lo[:, 0:1], bias_hi[:, :],
                                                ALU.mult, ALU.add))
            for j in range(J):
                rows = slice(32 * j, 32 * (j + 1))
                last = nc.vector.tensor_copy(bias_blocks[rows, j, :], bias_hi[rows, :])
                if j < J - 1:
                    link(last)
            last.then_inc(weights_ready, 1)

            def body(i, r, k):
                def one_hot(b, q):
                    dve.wait_ge(y_loaded[q % 2], 8 * (b - q % 2) + 16)
                    if late(i, b, 2):
                        dve.wait_ge(h_mm, b - 1)
                    nc.vector.tensor_scalar(onehot[q % 2][0:V, 1:S + 1], y_bc[q % 2][0:V, :], float(V - 1),
                                            vocab_id[0:V, 0:1], ALU.min, ALU.is_equal).then_inc(onehot_ready, 1)

                def aggregate(stats, mv, js, st_sem, mv_sem, at, lane):
                    dve.wait_ge(st_sem, at)
                    nc.vector.memset(idle[:, lane:lane + 1], 0.0)
                    for j in js:
                        last = nc.vector.bn_aggr(mv[:, j, :], stats[:, j, :])
                    last.then_inc(mv_sem, 1)

                def aggregate_1(b, q):
                    aggregate(stats1, mv1, range(J), st1_done, mv1_done, b + 1, 2)

                def aggregate_2(b, q, o):
                    aggregate(stats2, mv2, range(2 * o, 2 * o + 2), st2_done, mv2_done, b * 2 + o + 1, o)

                def stats_1(b, q, j):
                    if j == 0:
                        dve.wait_ge(h_relu, b + 1)
                    ins = nc.vector.bn_stats(stats1[:, j, :], h1[q][:, j, :])
                    if j == J - 1:
                        ins.then_inc(st1_done, 1)

                def shift_1(b, q):
                    dve.wait_ge(rstd1_done, b + 1)
                    nc.vector.scalar_tensor_tensor(shift1[:, :], mv1[:, :, 0], -1.0, rstd1[:, :], ALU.mult, ALU.mult)\
                      .then_inc(shift1_done, 1)

                def u1_lo(b, q):
                    dve.wait_ge(uthi_done, b + 1)
                    nc.vector.scalar_tensor_tensor(uT_lo[:, :], ps_a[:, :], LIFT, uT_hi[:, :],
                                                   ALU.mult, ALU.subtract).then_inc(utlo_done, 1)

                def p_lo(b, q):
                    dve.wait_ge(phi_done, b + 1)
                    nc.vector.scalar_tensor_tensor(pT_lo[:, :], ps_a[:, :], PROJ_SCALE, pT_hi[:, :],
                                                   ALU.mult, ALU.subtract).then_inc(plo_done, 1)

                def invert_sums(b, q, o):
                    dve.wait_ge(o_mm, b * 2 + o + 1)
                    nc.vector.reciprocal(inv_z[:, o, :], ps_o[o][:, D::O_STEP]).then_inc(invz_done, 1)

                def residual(b, q, o):
                    dve.wait_ge(invz_done, b * 2 + o + 1)
                    for n in range(2):
                        j = 2 * o + n
                        last = nc.vector.scalar_tensor_tensor(
                            h2[q % 2][:, j, :], ps_o[o][:, n * O_STEP:n * O_STEP + D], inv_z[:, o, n:n + 1],
                            h1[q][:, j, :], ALU.mult, ALU.add)
                    last.then_inc(h2_done, 1)

                def stats_2(b, q, o):
                    dve.wait_ge(h2_done, b * 2 + o + 1)
                    for j in range(2 * o, 2 * o + 2):
                        last = nc.vector.bn_stats(stats2[:, j, :], h2[q % 2][:, j, :])
                    last.then_inc(st2_done, 1)

                def norm_2(b, q):
                    dve.wait_ge(rstd2_done, b + 1)
                    if late(i, b):
                        dve.wait_ge(u2_mm, b)
                    for j in range(J):
                        last = nc.vector.tensor_scalar(u2[:, j, :], h2[q % 2][:, j, :], mv2[:, j, 0:1],
                                                       rstd2[:, j:j + 1], ALU.subtract, ALU.mult)
                    last.then_inc(u2_done, 1)

                def u2_lo(b, q):
                    dve.wait_ge(u2hi_done, b + 1)
                    nc.vector.scalar_tensor_tensor(u2T_lo[q % 2][:, :], ps_b[:, :], LIFT, u2T_hi[q % 2][:, :],
                                                   ALU.mult, ALU.subtract).then_inc(u2lo_done, 1)

                def over(x):
                    return x[:, :].unsqueeze(2).to_broadcast([P, J, E])

                def routing(b, q, n):
                    if n > 1:
                        dve.wait_ge(route, b * RD + n - 1)
                    if n == 1:
                        dve.wait_ge(g_mm, b + 1)
                        ins = nc.vector.scalar_tensor_tensor(
                            logits[:, :, :], ps_b[:, 0:J * E].rearrange("p (j e) -> p j e", j=J), unscale[:, 3:4],
                            router_gamma[:, :].unsqueeze(1).to_broadcast([P, J, E]), ALU.mult, ALU.add)
                    elif n == 2:
                        ins = nc.vector.tensor_reduce(top1[:, :], logits[:, :, :], AX.X, ALU.max)
                    elif n == 3:
                        ins = nc.vector.tensor_tensor(below[:, :, :], logits[:, :, :], over(top1), ALU.subtract)
                    elif n == 4:
                        ins = nc.vector.scalar_tensor_tensor(rank1[:, :, :], below[:, :, :], 0.0, first_wins[:, :, :],
                                                             ALU.is_equal, ALU.mult)
                    elif n == 5:
                        ins = nc.vector.tensor_reduce(best1[:, :], rank1[:, :, :], AX.X, ALU.max)
                    elif n == 6:
                        ins = nc.vector.tensor_tensor(pick1[:, :, :], rank1[:, :, :], over(best1), ALU.is_equal)
                    elif n == 7:
                        ins = nc.vector.scalar_tensor_tensor(rest[:, :, :], pick1[:, :, :], MASKED, below[:, :, :],
                                                             ALU.mult, ALU.add)
                    elif n == 8:
                        ins = nc.vector.tensor_reduce(top2[:, :], rest[:, :, :], AX.X, ALU.max)
                    elif n == 9:
                        ins = nc.vector.tensor_tensor(tied2[:, :, :], rest[:, :, :], over(top2), ALU.is_equal)
                    elif n == 10:
                        ins = nc.vector.tensor_tensor(rank2[:, :, :], tied2[:, :, :], first_wins[:, :, :], ALU.mult)
                    elif n == 11:
                        ins = nc.vector.tensor_reduce(best2[:, :], rank2[:, :, :], AX.X, ALU.max)
                    else:
                        ins = nc.vector.tensor_tensor(pick2[:, :, :], rank2[:, :, :], over(best2), ALU.is_equal)
                    ins.then_inc(route, 1)

                def softmax_sum(b, q):
                    dve.wait_ge(gexp_done, b + 1)
                    nc.vector.tensor_reduce(expo_sum[:, :], expo[:, :, :], AX.X, ALU.add).then_inc(zsum_done, 1)

                def softmax_inv(b, q):
                    dve.wait_ge(zsum_done, b + 1)
                    nc.vector.reciprocal(expo_inv[:, :], expo_sum[:, :]).then_inc(inv_done, 1)

                def start_acc(b, q):
                    dve.wait_ge(b_mm, b + 1)
                    if late(i, b, 2):
                        dve.wait_ge(fin_done, (b - 1) * J)
                    nc.vector.scalar_tensor_tensor(acc[q % 2][:, :, :].rearrange("p j d -> p (j d)"), ps_b[:, :],
                                                   unscale[:, 5:6], h2[q % 2][:, :, :].rearrange("p j d -> p (j d)"),
                                                   ALU.mult, ALU.add).then_inc(acc_init, 1)

                def add_expert(b, q, j, e):
                    if e == 0:
                        if j == 0:
                            dve.wait_ge(acc_init, b + 1)
                            dve.wait_ge(route_p, b * RP + RP)
                        dve.wait_ge(y_even_mm, b * J + j + 1)
                    else:
                        dve.wait_ge(acc_step, (b * J + j) * HE + e)
                    nc.vector.scalar_tensor_tensor(acc[q % 2][:, j, :], ps_y[0][:, e * D:(e + 1) * D],
                                                   combine_y[q % 2][:, j, e:e + 1], acc[q % 2][:, j, :],
                                                   ALU.mult, ALU.add).then_inc(acc_step, 1)

                now, in1, in2, in3, in4 = (has(i, n) for n in range(5))
                ago1, ago2, ago3, ago4 = (has(i, -n) for n in range(1, 5))
                if ago4:
                    add_expert(r - 4, k, 3, 0)
                    add_expert(r - 4, k, 3, 1)
                if in3:
                    one_hot(r + 3, (k + 3) % 4)
                if ago4:
                    add_expert(r - 4, k, 3, 2)
                    add_expert(r - 4, k, 3, 3)
                if ago2:
                    norm_2(r - 2, (k + 2) % 4)
                if ago3:
                    start_acc(r - 3, (k + 1) % 4)
                if in1:
                    stats_1(r + 1, (k + 1) % 4, 0)
                if ago3:
                    add_expert(r - 3, (k + 1) % 4, 0, 0)
                if in1:
                    stats_1(r + 1, (k + 1) % 4, 1)
                if ago3:
                    add_expert(r - 3, (k + 1) % 4, 0, 1)
                if in1:
                    stats_1(r + 1, (k + 1) % 4, 2)
                if ago3:
                    add_expert(r - 3, (k + 1) % 4, 0, 2)
                if in1:
                    stats_1(r + 1, (k + 1) % 4, 3)
                if ago3:
                    add_expert(r - 3, (k + 1) % 4, 0, 3)
                if ago2:
                    u2_lo(r - 2, (k + 2) % 4)
                if in1:
                    aggregate_1(r + 1, (k + 1) % 4)
                if now:
                    u1_lo(r, k)
                if ago3:
                    add_expert(r - 3, (k + 1) % 4, 1, 0)
                if ago2:
                    routing(r - 2, (k + 2) % 4, 1)
                if ago3:
                    add_expert(r - 3, (k + 1) % 4, 1, 1)
                if ago2:
                    routing(r - 2, (k + 2) % 4, 2)
                if ago3:
                    add_expert(r - 3, (k + 1) % 4, 1, 2)
                if ago2:
                    routing(r - 2, (k + 2) % 4, 3)
                if ago1:
                    invert_sums(r - 1, (k + 3) % 4, 0)
                if ago2:
                    routing(r - 2, (k + 2) % 4, 4)
                if ago3:
                    add_expert(r - 3, (k + 1) % 4, 1, 3)
                if ago2:
                    routing(r - 2, (k + 2) % 4, 5)
                    softmax_sum(r - 2, (k + 2) % 4)
                if in1:
                    shift_1(r + 1, (k + 1) % 4)
                if ago2:
                    routing(r - 2, (k + 2) % 4, 6)
                if ago1:
                    residual(r - 1, (k + 3) % 4, 0)
                if ago2:
                    routing(r - 2, (k + 2) % 4, 7)
                if now:
                    p_lo(r, k)
                if ago2:
                    routing(r - 2, (k + 2) % 4, 8)
                    softmax_inv(r - 2, (k + 2) % 4)
                    routing(r - 2, (k + 2) % 4, 9)
                if ago3:
                    add_expert(r - 3, (k + 1) % 4, 2, 0)
                if ago2:
                    routing(r - 2, (k + 2) % 4, 10)
                if ago3:
                    add_expert(r - 3, (k + 1) % 4, 2, 1)
                if ago2:
                    routing(r - 2, (k + 2) % 4, 11)
                if ago1:
                    invert_sums(r - 1, (k + 3) % 4, 1)
                if ago3:
                    add_expert(r - 3, (k + 1) % 4, 2, 2)
                if ago2:
                    routing(r - 2, (k + 2) % 4, 12)
                if ago1:
                    residual(r - 1, (k + 3) % 4, 1)
                if ago3:
                    add_expert(r - 3, (k + 1) % 4, 2, 3)
                if ago1:
                    stats_2(r - 1, (k + 3) % 4, 0)
                    stats_2(r - 1, (k + 3) % 4, 1)
                    aggregate_2(r - 1, (k + 3) % 4, 0)
                    aggregate_2(r - 1, (k + 3) % 4, 1)

            run(dve, body)

        @block.gpsimd
        def _(pool):
            count = [0]

            def link(ins):
                count[0] += 1
                ins.then_inc(pool_setup, 1)
                pool.wait_ge(pool_setup, count[0])

            nc.gpsimd.memset(amax[:, :], 0.0).then_inc(amax_zeroed, 1)
            link(nc.gpsimd.memset(sixteenth[:, :], 1.0 / NI))
            link(nc.gpsimd.memset(ident[:, :], 0.0))
            nc.gpsimd.affine_select(out=ident[:, :], in_=ident[:, :], compare_op=ALU.not_equal, fill=1.0, base=0,
                                    pattern=[[-1, P]], channel_multiplier=1).then_inc(consts_made, 1)
            pool.wait_ge(consts_made, 1)
            link(nc.gpsimd.tensor_copy(ident16[:, :], ident[:, :]))
            link(nc.gpsimd.memset(row_expert[:, :, :], 0.0))
            link(nc.gpsimd.memset(lo_rows[:, :, :], 0.0))
            link(nc.gpsimd.memset(bias_blocks[:, :, :], 0.0))
            link(nc.gpsimd.affine_select(out=row_expert[:, :, :], in_=row_expert[:, :, :], compare_op=ALU.not_equal,
                                         fill=1.0, base=0, pattern=[[-1, E], [-E, P // E]], channel_multiplier=1))
            nc.gpsimd.affine_select(out=lo_rows[:, :, :], in_=lo_rows[:, :, :], compare_op=ALU.not_equal,
                                    fill=1.0, base=-16, pattern=[[-32, J], [-1, 16]], channel_multiplier=1)\
              .then_inc(consts_made, 1)
            pool.wait_ge(amax_found, 4)
            nc.gpsimd.partition_all_reduce(amax_all[:, :], amax[:, :], P, ABSMAX).then_inc(amax_spread, 1)
            link(nc.gpsimd.iota(vocab_id[:, :], pattern=[[0, 1]], base=0, channel_multiplier=1,
                                allow_small_or_imprecise_dtypes=True))
            link(nc.gpsimd.iota(first_wins[:, :, :], pattern=[[0, J], [-1, E]], base=E, channel_multiplier=0,
                                allow_small_or_imprecise_dtypes=True))
            link(nc.gpsimd.memset(minus_half[:, :], -0.5))
            link(nc.gpsimd.memset(eps[:, :], EPS))
            link(nc.gpsimd.memset(lift[:, :], LIFT))
            link(nc.gpsimd.memset(cpack[:, :, :], 0.0))
            for n in range(2):
                link(nc.gpsimd.memset(onehot[n][:, 0:1], 0.0))
            for n in range(4):
                link(nc.gpsimd.memset(u1[n][:, :, D:D + 4], 1.0))
            pool.wait_ge(amax_found, 6)
            nc.gpsimd.partition_all_reduce(amax2_all[:, :], amax2[:, :], P, ABSMAX).then_inc(amax_spread, 1)

            def body(i, r, k):
                def rstd(mv, var, rs, mv_sem, at, var_sem, rs_sem, b):
                    pool.wait_ge(mv_sem, at)
                    nc.gpsimd.tensor_tensor(var[:, :], mv[:, :, 1], eps[:, :], ALU.add)\
                      .then_inc(var_sem, 1)
                    pool.wait_ge(var_sem, b + 1)
                    nc.gpsimd.tensor_tensor(rs[:, :], var[:, :], minus_half[:, :], ALU.pow).then_inc(rs_sem, 1)

                def rstd_1(b, q):
                    rstd(mv1, var1, rstd1, mv1_done, b + 1, var1_done, rstd1_done, b)

                def rstd_2(b, q):
                    rstd(mv2, var2, rstd2, mv2_done, b * 2 + 2, var2_done, rstd2_done, b)

                def combine_weights(b, q):
                    at = [0]

                    def step(ins):
                        at[0] += 1
                        ins.then_inc(route_p, 1)
                        pool.wait_ge(route_p, b * RP + at[0])

                    def over(x):
                        return x.unsqueeze(2).to_broadcast([P, J, E])

                    pool.wait_ge(route, b * RD + 12)
                    step(nc.gpsimd.tensor_tensor(picks[:, :, :], pick1[:, :, :], pick2[:, :, :], ALU.add))
                    pool.wait_ge(gexp_done, b + 1)
                    step(nc.gpsimd.tensor_tensor(picked[:, :, :], picks[:, :, :], expo[:, :, :], ALU.mult))
                    pool.wait_ge(inv_done, b + 1)
                    step(nc.gpsimd.tensor_tensor(inv_lift[:, :], expo_inv[:, :], lift[:, :], ALU.mult))
                    step(nc.gpsimd.tensor_tensor(combine[:, :, :], picked[:, :, :], over(inv_lift[:, :]), ALU.mult))
                    if late(i, b):
                        pool.wait_ge(ct_mm, b)
                    step(nc.gpsimd.tensor_tensor(
                        cpack[:, :, :].rearrange("p j (h e) -> p j h e", h=2)[:, :, :, 0:E],
                        picked[:, :, :].unsqueeze(2).to_broadcast([P, J, 2, E]),
                        inv_lift[:, :].unsqueeze(2).unsqueeze(3).to_broadcast([P, J, 2, E]), ALU.mult))
                    step(nc.gpsimd.tensor_tensor(cpack[:, :, E:2 * E], combine[:, :, :], cpack[:, :, 0:E],
                                                 ALU.subtract))
                    if late(i, b, 2):
                        pool.wait_ge(acc_step, (b - 1) * J * HE)
                    step(nc.gpsimd.tensor_tensor(combine_y[q % 2][:, :, :], combine[:, :, :],
                                                 unscale[:, 4:5].unsqueeze(2).to_broadcast([P, J, E]), ALU.mult))

                def sum_odd(b, q, j):
                    at = (b * J + j) * 2
                    pool.wait_ge(y_odd_done, b * J + j + 1)
                    y = y_odd[j % 2]
                    nc.gpsimd.tensor_tensor(sum2[j % 2][:, :, :], y[:, 0:2, :], y[:, 2:4, :], ALU.add).then_inc(y_sum, 1)
                    pool.wait_ge(y_sum, at + 1)
                    nc.gpsimd.tensor_tensor(sum1[j % 2][:, :], sum2[j % 2][:, 0, :], sum2[j % 2][:, 1, :], ALU.add).then_inc(y_sum, 1)

                def finish(b, q, j):
                    pool.wait_ge(y_sum, (b * J + j + 1) * 2)
                    pool.wait_ge(acc_step, (b * J + j + 1) * HE)
                    if j == 0 and late(i, b, 2):
                        pool.wait_ge(out_stored[q % 2], 8 * (b - q % 2))
                    nc.gpsimd.tensor_tensor(out_sb[q % 2][:, j, :], acc[q % 2][:, j, :], sum1[j % 2][:, :], ALU.add)\
                      .then_inc(fin_done, 1)

                now, in1, in2, in3, in4 = (has(i, n) for n in range(5))
                ago1, ago2, ago3, ago4 = (has(i, -n) for n in range(1, 5))
                if ago4:
                    finish(r - 4, k, 3)
                if ago3:
                    sum_odd(r - 3, (k + 1) % 4, 1)
                if ago2:
                    combine_weights(r - 2, (k + 2) % 4)
                if ago1:
                    rstd_2(r - 1, (k + 3) % 4)
                if ago3:
                    finish(r - 3, (k + 1) % 4, 0)
                    finish(r - 3, (k + 1) % 4, 1)
                    sum_odd(r - 3, (k + 1) % 4, 2)
                    sum_odd(r - 3, (k + 1) % 4, 3)
                    finish(r - 3, (k + 1) % 4, 2)
                if ago2:
                    sum_odd(r - 2, (k + 2) % 4, 0)
                if in2:
                    rstd_1(r + 2, (k + 2) % 4)

            pool.wait_ge(weights_ready, 1)
            run(pool, body)


_INS = ['x', 'L0_tok_emb_weight', 'L0_tok_conv_weight', 'L0_attn_attention_weights', 'L0_ffn_Ins_tk',
        'L0_ffn_gate_w', 'L0_ffn_expert_w', 'L0_ffn_expert_b', 'L0_ffn_gamma_w', 'L0_ffn_beta_w', 'L0_ffn_rmod_w']


def kernel(**inputs):
    import numpy as _np
    import concourse.bacc as _bacc
    from concourse import mybir as _mybir
    from concourse.bass_utils import run_bass_kernel_spmd as _run

    nc = _bacc.Bacc("TRN2", target_bir_lowering=False, num_devices=1)
    arrays, args = {}, []
    for name in _INS:
        a = _np.ascontiguousarray(inputs[name])
        arrays[f"in_{name}_dram"] = a
        args.append(nc.dram_tensor(f"in_{name}_dram", a.shape, _mybir.dt.from_np(a.dtype), kind="ExternalInput").ap())
    batch, seq = inputs['x'].shape
    width = inputs['L0_tok_emb_weight'].shape[1]
    args.append(nc.dram_tensor("out_dram", (batch, seq, width), _mybir.dt.float32, kind="ExternalOutput").ap())
    tower_kernel(nc, *args)
    r = _run(nc, [arrays], core_ids=[0])
    return r.results[0]["out_dram"]
```

```python
import concourse.bass as bass
from concourse import mybir
from contextlib import ExitStack


def tower_kernel(
    nc: bass.Bass,
    tokens: bass.AP,
    emb_weight: bass.AP,
    conv_weight: bass.AP,
    attn_weight: bass.AP,
    instructions: bass.AP,
    gate_weight: bass.AP,
    expert_weight: bass.AP,
    expert_bias: bass.AP,
    gamma_weight: bass.AP,
    beta_weight: bass.AP,
    rmod_weight: bass.AP,
    out: bass.AP,
):
    fp32 = mybir.dt.float32
    fp16 = mybir.dt.float16
    i32 = mybir.dt.int32
    ALU = mybir.AluOpType
    ACT = mybir.ActivationFunctionType
    AX = mybir.AxisListType
    ABSMAX = bass.bass_isa.ReduceOp.absmax

    B, S = tokens.shape
    V, D = emb_weight.shape
    E = gate_weight.shape[1]
    NI = instructions.shape[1]
    P = 128
    J = S // P
    HE = E // 2
    EPS = 1e-5
    QMAX = 127.0
    ROUND = 12582912.0
    LIFT = 1024.0
    TINY = 1e-30
    EXPONENT_BITS = 0x7F800000
    PROJ_SCALE = 2.0 ** -14
    MASKED = -1e30
    WARM_UP = 15

    y_rows = tokens
    out_rows = out.rearrange("b (p j) d -> b p j d", j=J)

    ctx = ExitStack()
    with ctx:
        def sb(name, shape, dt):
            return ctx.enter_context(nc.sbuf_tensor(name, shape, dt))

        def sem(name):
            return ctx.enter_context(nc.semaphore(name))

        emb = sb("emb", [P, D], fp32)
        conv = sb("conv", [P, D * 2], fp32)
        conv_q = sb("conv_q", [P, D * 2], fp32)
        emb_q = sb("emb_q", [P, D], fp32)
        table = sb("table", [P, 2, D], fp32)
        table_hi = sb("table_hi", [P, 2, D], fp16)
        table_lo = sb("table_lo", [P, 2, D], fp16)
        attn_w = sb("attn_w", [P, D], fp32)
        attn_hi = sb("attn_hi", [P, D], fp16)
        attn_lo = sb("attn_lo", [P, D], fp16)
        gate_w = sb("gate_w", [P, E], fp32)
        gate_hi = sb("gate_hi", [P, E], fp16)
        gate_lo = sb("gate_lo", [P, E], fp16)
        expert_w = sb("expert_w", [P, E, D], fp32)
        expert_hi = sb("expert_hi", [P, E, D], fp16)
        expert_lo = sb("expert_lo", [P, E, D], fp16)
        expert_b = sb("expert_b", [E, D], fp32)
        beta_w = sb("beta_w", [P, E, D], fp32)
        gamma_w = sb("gamma_w", [E, D], fp32)
        gamma_t = sb("gamma_t", [P, E], fp32)
        rmod_w = sb("rmod_w", [P, E], fp32)
        ins_w = sb("ins_w", [NI, D], fp32)
        ins_mean = sb("ins_mean", [P, P], fp32)
        mean_of = sb("mean_of", [P, E, P], fp32)
        gam_of = sb("gam_of", [E, P], fp32)
        column_of = sb("column_of", [P, E, P], fp32)
        own_column = sb("own_column", [E, P], fp32)
        sixteenth = sb("sixteenth", [NI, P], fp32)
        router_gamma = sb("router_gamma", [P, E], fp32)
        gam = sb("gam", [P, E], fp32)
        bias_row = sb("bias_row", [P, D], fp32)
        bias_hi = sb("bias_hi", [P, D], fp16)
        bias_lo = sb("bias_lo", [P, D], fp16)
        bias_blocks = sb("bias_blocks", [P, J, D], fp16)
        lo_rows = sb("lo_rows", [P, J, 16], fp32)
        is_lo = sb("is_lo", [P, 1], fp32)
        is_hi = sb("is_hi", [P, 1], fp32)
        amax = sb("amax", [P, 2], fp32)
        amax_all = sb("amax_all", [P, 2], fp32)
        amax2 = sb("amax2", [P, 2], fp32)
        amax2_all = sb("amax2_all", [P, 2], fp32)
        amax3 = sb("amax3", [P, 2], fp32)
        amax3_all = sb("amax3_all", [P, 2], fp32)
        step_of = sb("step_of", [P, 6], fp32)
        inv_step = sb("inv_step", [P, 6], fp32)
        unscale = sb("unscale", [P, 6], fp32)
        h_scale = sb("h_scale", [P, 1], fp32)
        vocab_id = sb("vocab_id", [P, 1], fp32)
        first_wins = sb("first_wins", [P, J, E], fp32)
        minus_half = sb("minus_half", [P, J], fp32)
        idle = sb("idle", [P, 3], fp32)
        eps = sb("eps", [P, J], fp32)
        lift = sb("lift", [P, J], fp32)
        ident = sb("ident", [P, P], fp32)
        ident16 = sb("ident16", [P, P], fp16)
        warm = sb("warm", [P, 512], fp16)

        y_bc = [sb(f"y_bc{n}", [P, S], i32) for n in range(4)]
        onehot = [sb(f"onehot{n}", [P, S + 1], fp16) for n in range(2)]
        h1 = [sb(f"h1_{n}", [P, J, D], fp32) for n in range(4)]
        u1 = [sb(f"u1_{n}", [P, J, D + 4], fp32) for n in range(4)]
        shift1 = sb("shift1", [P, J], fp32)
        stats1 = sb("stats1", [P, J, 6], fp32)
        mv1 = sb("mv1", [P, J, 2], fp32)
        var1 = sb("var1", [P, J], fp32)
        rstd1 = sb("rstd1", [P, J], fp32)
        uT_hi = sb("uT_hi", [P, S], fp16)
        uT_lo = sb("uT_lo", [P, S], fp16)
        pT_hi = sb("pT_hi", [P, S], fp16)
        pT_lo = sb("pT_lo", [P, S], fp16)
        th = [sb(f"th{n}", [P, S], fp32) for n in range(2)]
        probs = sb("probs", [P, J, S], fp32)
        inv_z = sb("inv_z", [P, 2, 2], fp32)
        h2 = [sb(f"h2_{n}", [P, J, D], fp32) for n in range(2)]
        stats2 = sb("stats2", [P, J, 6], fp32)
        mv2 = sb("mv2", [P, J, 2], fp32)
        var2 = sb("var2", [P, J], fp32)
        rstd2 = sb("rstd2", [P, J], fp32)
        u2 = sb("u2", [P, J, D], fp32)
        u2T_hi = [sb(f"u2T_hi{n}", [P, S], fp16) for n in range(2)]
        u2T_lo = [sb(f"u2T_lo{n}", [P, S], fp16) for n in range(2)]
        logits = sb("logits", [P, J, E], fp32)
        top1 = sb("top1", [P, J], fp32)
        below = sb("below", [P, J, E], fp32)
        expo = sb("expo", [P, J, E], fp32)
        expo_sum = sb("expo_sum", [P, J], fp32)
        expo_inv = sb("expo_inv", [P, J], fp32)
        inv_lift = sb("inv_lift", [P, J], fp32)
        rank1 = sb("rank1", [P, J, E], fp32)
        best1 = sb("best1", [P, J], fp32)
        pick1 = sb("pick1", [P, J, E], fp32)
        rest = sb("rest", [P, J, E], fp32)
        top2 = sb("top2", [P, J], fp32)
        tied2 = sb("tied2", [P, J, E], fp32)
        rank2 = sb("rank2", [P, J, E], fp32)
        best2 = sb("best2", [P, J], fp32)
        pick2 = sb("pick2", [P, J, E], fp32)
        picks = sb("picks", [P, J, E], fp32)
        picked = sb("picked", [P, J, E], fp32)
        combine = sb("combine", [P, J, E], fp32)
        combine_y = [sb(f"combine_y{n}", [P, J, E], fp32) for n in range(2)]
        cpack = sb("cpack", [P, J, 32], fp16)
        cT = sb("cT", [P, P], fp16)
        acc = [sb(f"acc{n}", [P, J, D], fp32) for n in range(2)]
        y_odd = [sb(f"y_odd{n}", [P, HE, D], fp32) for n in range(2)]
        sum2 = [sb(f"sum2_{n}", [P, 2, D], fp32) for n in range(2)]
        sum1 = [sb(f"sum1_{n}", [P, D], fp32) for n in range(2)]
        out_sb = [sb(f"out_sb{n}", [P, J, D], fp32) for n in range(2)]

        def bank(name):
            return ctx.enter_context(nc.psum_tensor(name, [P, 512], fp32))

        ps_s = [bank(f"ps_s{n}") for n in range(2)]
        ps_y = [bank(f"ps_y{n}") for n in range(2)]
        ps_o = [bank(f"ps_o{n}") for n in range(2)]
        ps_a = bank("ps_a")
        ps_b = bank("ps_b")
        O_STEP = 256

        loaded = {n: sem(f"loaded_{n}") for n in ("emb", "conv", "attn", "gate", "expert", "bias", "beta", "small")}
        amax_zeroed = sem("amax_zeroed")
        warm_made = sem("warm_made")
        consts_made = sem("consts_made")
        tokens_made = sem("tokens_made")
        amax_spread = sem("amax_spread")
        pool_setup = sem("pool_setup")
        dve_setup = sem("dve_setup")
        amax_found = sem("amax_found")
        amax2_found = sem("amax2_found")
        amax3_found = sem("amax3_found")
        means_out = sem("means_out")
        gam_masked = sem("gam_masked")
        means_mm = sem("means_mm")
        table_ready = sem("table_ready")
        attn_ready = sem("attn_ready")
        gate_ready = sem("gate_ready")
        experts_ready = sem("experts_ready")
        y_loaded = [sem(f"y_loaded{n}") for n in range(4)]
        out_stored = [sem(f"out_stored{n}") for n in range(2)]
        onehot_ready = sem("onehot_ready")
        h_mm = sem("h_mm")
        h_relu = sem("h_relu")
        st1_done = sem("st1_done")
        mv1_done = sem("mv1_done")
        var1_done = sem("var1_done")
        rstd1_done = sem("rstd1_done")
        shift1_done = sem("shift1_done")
        u1_done = sem("u1_done")
        t_mm = sem("t_mm")
        uthi_done = sem("uthi_done")
        utlo_done = sem("utlo_done")
        p_mm = sem("p_mm")
        phi_done = sem("phi_done")
        plo_done = sem("plo_done")
        s_mm = sem("s_mm")
        tanh_done = sem("tanh_done")
        exp_done = sem("exp_done")
        o_mm = sem("o_mm")
        invz_done = sem("invz_done")
        h2_done = sem("h2_done")
        st2_done = sem("st2_done")
        mv2_done = sem("mv2_done")
        var2_done = sem("var2_done")
        rstd2_done = sem("rstd2_done")
        u2_done = sem("u2_done")
        u2_mm = sem("u2_mm")
        u2hi_done = sem("u2hi_done")
        u2lo_done = sem("u2lo_done")
        g_mm = sem("g_mm")
        route = sem("route")
        gexp_done = sem("gexp_done")
        route_p = sem("route_p")
        zsum_done = sem("zsum_done")
        inv_done = sem("inv_done")
        ct_mm = sem("ct_mm")
        ct_done = sem("ct_done")
        b_mm = sem("b_mm")
        acc_init = sem("acc_init")
        y_even_mm = sem("y_even_mm")
        y_odd_mm = sem("y_odd_mm")
        acc_step = sem("acc_step")
        y_odd_done = sem("y_odd_done")
        y_sum = sem("y_sum")
        fin_done = sem("fin_done")

        RD = 12
        RP = 7
        RP_PACKED = 6

        UNROLL = 4
        LOOP_FROM, LOOP_TO = 8, 28
        FIRST_ROUND, END_ROUND = -4, B + 4
        SPARE_FROM = B - 2

        def run(eng, body):
            for r in range(FIRST_ROUND, LOOP_FROM):
                body(r, r, r % UNROLL)
            with eng.Fori(LOOP_FROM // UNROLL, LOOP_TO // UNROLL) as turn:
                for k in range(UNROLL):
                    body(None, turn * UNROLL + k, k)
            for r in range(LOOP_TO, END_ROUND):
                body(r, r, r % UNROLL)

        def has(i, n):
            return i is None or 0 <= i + n < B

        def late(i, b, n=1):
            return i is None or b >= n

        def spare(i, b):
            return i is not None and b >= SPARE_FROM

        def y_bank(i, b, j, half):
            return ps_s[half] if spare(i, b) and j % 2 else ps_y[half]

        block = ctx.enter_context(nc.Block())

        @block.sync
        def _(sp):
            sp.dma_start(emb[0:V, :], emb_weight).then_inc(loaded["emb"], 16)
            sp.dma_start(conv[:, :], conv_weight.rearrange("d o k -> (d o k)").partition_broadcast(P))\
              .then_inc(loaded["conv"], 16)
            sp.dma_start(y_bc[0][0:V, :], y_rows[0, :].partition_broadcast(V)).then_inc(y_loaded[0], 16)
            sp.dma_start(attn_w[:, :], attn_weight).then_inc(loaded["attn"], 16)
            sp.dma_start(gate_w[:, :], gate_weight).then_inc(loaded["gate"], 16)
            sp.dma_start(y_bc[1][0:V, :], y_rows[1, :].partition_broadcast(V)).then_inc(y_loaded[1], 16)
            for n in range(2, 4):
                sp.dma_start(y_bc[n][0:V, :], y_rows[n, :].partition_broadcast(V)).then_inc(y_loaded[n], 16)
            sp.dma_start(ins_w[:, :], instructions[0, :, :]).then_inc(loaded["small"], 16)
            sp.dma_start(gamma_w[:, :], gamma_weight).then_inc(loaded["small"], 16)
            sp.dma_start(rmod_w[:, :], rmod_weight).then_inc(loaded["small"], 16)
            sp.dma_start(expert_b[:, :], expert_bias).then_inc(loaded["bias"], 16)
            sp.dma_start(expert_w[:, :, :], expert_weight.rearrange("e l d -> l e d")).then_inc(loaded["expert"], 16)
            sp.dma_start(beta_w[:, :, :], beta_weight.rearrange("e h d -> h e d")).then_inc(loaded["beta"], 16)

            def body(i, r, k):
                if has(i, 4) and late(i, r + 4, 4):
                    sp.wait_ge(onehot_ready, r + 1)
                    sp.dma_start(y_bc[k][0:V, :], y_rows[r + 4, :].partition_broadcast(V))\
                      .then_inc(y_loaded[k], 16)
                if has(i, -3):
                    sp.wait_ge(fin_done, (r - 3) * J + J)
                    sp.dma_start(out_rows[r - 3, :, :, :], out_sb[(k + 3) % 2][:, :, :])\
                      .then_inc(out_stored[(k + 3) % 2], 16)

            run(sp, body)
            for n in range(2):
                sp.wait_ge(out_stored[n], 16 * (B // 2))

        @block.tensor
        def _(pe):
            def keep_warm(count):
                for n in range(count):
                    nc.tensor.matmul(ps_s[1][:, :], warm[:, 0:P], warm[:, :], start=True, stop=True)

            def mean_products():
                pe.wait_ge(loaded["small"], 48)
                pe.wait_ge(consts_made, 1)
                nc.tensor.matmul(ps_y[0][:, 0:P], ins_w[:, :], sixteenth[:, :], start=True, stop=True)\
                  .then_inc(means_mm, 1)
                nc.tensor.transpose(ps_y[1][:, 0:E], gamma_w[:, :], ident[0:E, 0:E]).then_inc(means_mm, 1)
                pe.wait_ge(means_out, 2)
                nc.tensor.matmul(ps_b[:, 0:E], ins_mean[:, :], rmod_w[:, :], start=True, stop=True)
                nc.tensor.matmul(ps_b[:, E:2 * E], ins_mean[:, :], gamma_t[:, :], start=True, stop=True)
                nc.tensor.matmul(ps_b[0:E, P:2 * P], gamma_t[:, :], ins_mean[:, :], start=True, stop=True)\
                  .then_inc(means_mm, 1)

            def bias_products():
                pe.wait_ge(means_out, 4)
                pe.wait_ge(loaded["beta"], 16)
                pe.wait_ge(loaded["bias"], 16)
                for e in range(E):
                    nc.tensor.matmul(ps_y[0][:, 0:D], mean_of[:, e, :], beta_w[:, e, :], start=(e == 0), stop=False)
                pe.wait_ge(gam_masked, 1)
                nc.tensor.matmul(ps_y[0][:, 0:D], gam_of[:, :], expert_b[:, :], start=False, stop=True)\
                  .then_inc(means_mm, 1)

            def body(i, r, k):
                def scores(b, q, t):
                    if t == 0:
                        pe.wait_ge(plo_done, b + 1)
                    if t >= 2 or late(i, b):
                        pe.wait_ge(tanh_done, b * J + t - 1)
                    for n, (a, c) in enumerate(((uT_hi, pT_hi), (uT_hi, pT_lo), (uT_lo, pT_hi))):
                        last = nc.tensor.matmul(ps_s[t % 2][:, :], a[:, t * P:(t + 1) * P], c[:, :],
                                                start=(n == 0), stop=(n == 2))
                    last.then_inc(s_mm, 1)

                def attend(b, q, s):
                    if s == 0:
                        pe.wait_ge(exp_done, b * J + J)
                    if s % 2 == 0 and late(i, b):
                        pe.wait_ge(h2_done, b * 2 - 1 + s // 2)
                    o = ps_o[s // 2][:, (s % 2) * O_STEP:(s % 2) * O_STEP + D + 1]
                    for t in range(J):
                        last = nc.tensor.matmul(o, probs[:, t, s * P:(s + 1) * P], u1[q][:, t, 0:D + 1],
                                                start=(t == 0), stop=(t == J - 1))
                    if s % 2:
                        last.then_inc(o_mm, 1)

                def embed(b, q):
                    if i is not None and b == 0:
                        pe.wait_ge(table_ready, 1)
                    pe.wait_ge(onehot_ready, b + 1)
                    if late(i, b, 2):
                        pe.wait_ge(plo_done, b - 1)
                    elif b == 1:
                        pe.wait_ge(h_relu, 1)
                    for j in range(J):
                        n = 0
                        for tap in range(2):
                            toks = onehot[q % 2][0:V, tap + j:tap + j + J * (P - 1) + 1:J]
                            for part in (table_hi, table_lo):
                                last = nc.tensor.matmul(ps_a[:, j * D:(j + 1) * D], toks, part[0:V, tap, :],
                                                        start=(n == 0), stop=(n == 3))
                                n += 1
                    last.then_inc(h_mm, 1)

                def turn_u1(b, q):
                    pe.wait_ge(u1_done, b + 1)
                    if i is None or b + 1 < B:
                        pe.wait_ge(h_relu, b + 2)
                    for j in range(J):
                        last = nc.tensor.transpose(ps_a[:, j * P:(j + 1) * P], u1[q][:, j, 0:D], ident[:, :])
                    last.then_inc(t_mm, 1)

                def project(b, q):
                    if i is not None and b == 0:
                        pe.wait_ge(attn_ready, 1)
                    pe.wait_ge(utlo_done, b + 1)
                    for n, (a, c) in enumerate(((attn_hi, uT_hi), (attn_hi, uT_lo), (attn_lo, uT_hi))):
                        last = nc.tensor.matmul(ps_a[:, :], a[:, :], c[:, :], start=(n == 0), stop=(n == 2))
                    last.then_inc(p_mm, 1)

                def turn_u2(b, q):
                    pe.wait_ge(u2_done, b + 1)
                    if late(i, b):
                        pe.wait_ge(acc_init, b)
                    for j in range(J):
                        last = nc.tensor.transpose(ps_b[:, j * P:(j + 1) * P], u2[:, j, :], ident[:, :])
                    last.then_inc(u2_mm, 1)

                def gate(b, q):
                    if i is not None and b == 0:
                        pe.wait_ge(gate_ready, 1)
                    pe.wait_ge(u2lo_done, b + 1)
                    for j in range(J):
                        rows = slice(j * P, (j + 1) * P)
                        for n, (a, c) in enumerate(((u2T_hi, gate_hi), (u2T_hi, gate_lo), (u2T_lo, gate_hi))):
                            last = nc.tensor.matmul(ps_b[:, j * E:(j + 1) * E], a[q % 2][:, rows], c[:, :],
                                                    start=(n == 0), stop=(n == 2))
                    last.then_inc(g_mm, 1)

                def turn_combine(b, q):
                    if i is not None and b == 0:
                        pe.wait_ge(consts_made, 2)
                    pe.wait_ge(route_p, b * RP + RP_PACKED)
                    nc.tensor.transpose(ps_b[:, 0:P // 2].bitcast(fp16), cpack[:, :, :].rearrange("p j c -> p (j c)"),
                                        ident16[:, :]).then_inc(ct_mm, 1)

                def bias_rows(b, q):
                    if i is not None and b == 0:
                        pe.wait_ge(experts_ready, 1)
                    pe.wait_ge(ct_done, b + 1)
                    nc.tensor.matmul(ps_b[:, :], cT[:, :], bias_blocks[:, :, :], start=True, stop=True)\
                      .then_inc(b_mm, 1)

                def experts(b, q, j, half):
                    if i is not None and b == 0 and j == 0:
                        pe.wait_ge(experts_ready, 1)
                    if spare(i, b) and b == SPARE_FROM and j == 1:
                        pe.wait_ge(tanh_done, B * J)
                    elif spare(i, b) and (b > SPARE_FROM or j > 1):
                        if half:
                            pe.wait_ge(y_odd_done, b * J + j - 1)
                        else:
                            pe.wait_ge(acc_step, (b * J + j - 1) * HE)
                    elif j > 0 or late(i, b):
                        if half:
                            pe.wait_ge(y_odd_done, b * J + j)
                        else:
                            pe.wait_ge(acc_step, (b * J + j) * HE)
                    rows = slice(j * P, (j + 1) * P)
                    es = slice(half * HE, (half + 1) * HE)
                    for n, (a, c) in enumerate(((u2T_hi, expert_hi), (u2T_hi, expert_lo), (u2T_lo, expert_hi))):
                        last = nc.tensor.matmul(y_bank(i, b, j, half)[:, :], a[q % 2][:, rows], c[:, es, :],
                                                start=(n == 0), stop=(n == 2))
                    last.then_inc(y_odd_mm if half else y_even_mm, 1)

                ago3, ago2, ago1, now, in2 = (has(i, n) for n in (-3, -2, -1, 0, 2))
                if now:
                    turn_u1(r, k)
                    if i == 0:
                        bias_products()
                if ago2:
                    turn_u2(r - 2, (k + 2) % 4)
                if ago1:
                    attend(r - 1, (k + 3) % 4, 0)
                if ago3:
                    experts(r - 3, (k + 1) % 4, 1, 1)
                    experts(r - 3, (k + 1) % 4, 1, 0)
                if ago2:
                    gate(r - 2, (k + 2) % 4)
                if ago1:
                    attend(r - 1, (k + 3) % 4, 1)
                if ago3:
                    experts(r - 3, (k + 1) % 4, 2, 1)
                if now:
                    project(r, k)
                    if i == 0:
                        keep_warm(6)
                if ago1:
                    attend(r - 1, (k + 3) % 4, 2)
                if ago3:
                    experts(r - 3, (k + 1) % 4, 2, 0)
                if ago1:
                    attend(r - 1, (k + 3) % 4, 3)
                if ago3:
                    experts(r - 3, (k + 1) % 4, 3, 1)
                if now:
                    scores(r, k, 0)
                    scores(r, k, 1)
                if ago3:
                    experts(r - 3, (k + 1) % 4, 3, 0)
                if in2:
                    embed(r + 2, (k + 2) % 4)
                    if i == -2:
                        mean_products()
                    if i == -1:
                        keep_warm(8)
                if now:
                    scores(r, k, 2)
                if ago2:
                    turn_combine(r - 2, (k + 2) % 4)
                if now:
                    scores(r, k, 3)
                if ago2:
                    experts(r - 2, (k + 2) % 4, 0, 1)
                    bias_rows(r - 2, (k + 2) % 4)
                    experts(r - 2, (k + 2) % 4, 0, 0)

            pe.wait_ge(warm_made, 1)
            keep_warm(WARM_UP)
            run(pe, body)

        @block.scalar
        def _(act):
            act.wait_ge(means_mm, 1)
            nc.scalar.activation(ins_mean[:, :], ps_y[0][:, 0:P], ACT.Copy).then_inc(means_out, 1)
            act.wait_ge(means_mm, 2)
            nc.scalar.activation(gamma_t[:, :], ps_y[1][:, 0:E], ACT.Copy).then_inc(means_out, 1)
            def mask_means():
                act.wait_ge(means_out, 1)
                act.wait_ge(consts_made, 2)
                for n in range(2):
                    es = slice(n * HE, (n + 1) * HE)
                    nc.scalar.activation(mean_of[:, es, :], column_of[:, es, :], ACT.Copy, scale=ins_mean[:, 0:1])\
                      .then_inc(means_out, 1)

            def body(i, r, k):
                def tanh(b, q, t):
                    if i is not None and b == 0 and t == 0:
                        act.wait_ge(attn_ready, 1)
                    act.wait_ge(s_mm, b * J + t + 1)
                    if t >= 2 or late(i, b):
                        act.wait_ge(exp_done, b * J + t - 1)
                    nc.scalar.activation(th[t % 2][:, :], ps_s[t % 2][:, :], ACT.Tanh, scale=unscale[:, 2:3])\
                      .then_inc(tanh_done, 1)

                def exp(b, q, t):
                    act.wait_ge(tanh_done, b * J + t + 1)
                    if t == 0 and late(i, b):
                        act.wait_ge(o_mm, b * 2)
                    nc.scalar.activation(probs[:, t, :], th[t % 2][:, :], ACT.Exp).then_inc(exp_done, 1)

                def relu(b, q):
                    if i is not None and b == 0:
                        act.wait_ge(table_ready, 1)
                    act.wait_ge(h_mm, b + 1)
                    if late(i, b, 4):
                        act.wait_ge(h2_done, (b - 4) * 2 + 2)
                    nc.scalar.activation(h1[q][:, :, :], ps_a[:, :].rearrange("p (j d) -> p j d", j=J), ACT.Relu,
                                         scale=h_scale[:, 0:1]).then_inc(h_relu, 1)

                def norm_1(b, q):
                    act.wait_ge(shift1_done, b + 1)
                    if late(i, b, 4):
                        act.wait_ge(o_mm, (b - 4) * 2 + 2)
                    for j in range(J):
                        last = nc.scalar.activation(u1[q][:, j, 0:D], h1[q][:, j, :], ACT.Identity,
                                                    bias=shift1[:, j:j + 1], scale=rstd1[:, j:j + 1])
                    last.then_inc(u1_done, 1)

                def u1_hi(b, q):
                    act.wait_ge(t_mm, b + 1)
                    if late(i, b):
                        act.wait_ge(s_mm, b * J)
                    nc.scalar.activation(uT_hi[:, :], ps_a[:, :], ACT.Copy, scale=LIFT).then_inc(uthi_done, 1)

                def p_hi(b, q):
                    act.wait_ge(p_mm, b + 1)
                    nc.scalar.activation(pT_hi[:, :], ps_a[:, :], ACT.Copy, scale=PROJ_SCALE).then_inc(phi_done, 1)

                def u2_hi(b, q):
                    act.wait_ge(u2_mm, b + 1)
                    if late(i, b, 2):
                        act.wait_ge(y_even_mm, (b - 1) * J)
                    nc.scalar.activation(u2T_hi[q % 2][:, :], ps_b[:, :], ACT.Copy, scale=LIFT).then_inc(u2hi_done, 1)

                def gate_exp(b, q):
                    act.wait_ge(route, b * RD + 3)
                    nc.scalar.activation(expo[:, :, :], below[:, :, :], ACT.Exp).then_inc(gexp_done, 1)

                def c_out(b, q):
                    act.wait_ge(ct_mm, b + 1)
                    if late(i, b):
                        act.wait_ge(b_mm, b)
                    nc.scalar.activation(cT[:, :], ps_b[:, 0:P // 2].bitcast(fp16), ACT.Copy).then_inc(ct_done, 1)

                def y_out(b, q, j):
                    act.wait_ge(y_odd_mm, b * J + j + 1)
                    if j == 0:
                        act.wait_ge(route_p, b * RP + RP)
                    if j >= 2 or late(i, b):
                        act.wait_ge(y_sum, (b * J + j - 1) * 2 - 1)
                    for e in range(HE):
                        last = nc.scalar.activation(y_odd[j % 2][:, e, :], y_bank(i, b, j, 1)[:, e * D:(e + 1) * D],
                                                    ACT.Copy,
                                                    scale=combine_y[q % 2][:, j, HE + e:HE + e + 1])
                    last.then_inc(y_odd_done, 1)

                ago3, ago2, now, in1, in2 = (has(i, n) for n in (-3, -2, 0, 1, 2))
                if ago3:
                    y_out(r - 3, (k + 1) % 4, 0)
                if ago2:
                    u2_hi(r - 2, (k + 2) % 4)
                if now:
                    u1_hi(r, k)
                if ago3:
                    y_out(r - 3, (k + 1) % 4, 1)
                if ago2:
                    gate_exp(r - 2, (k + 2) % 4)
                if now:
                    p_hi(r, k)
                if ago3:
                    y_out(r - 3, (k + 1) % 4, 2)
                if in1:
                    norm_1(r + 1, (k + 1) % 4)
                if ago3:
                    y_out(r - 3, (k + 1) % 4, 3)
                if now:
                    tanh(r, k, 0)
                    tanh(r, k, 1)
                    exp(r, k, 0)
                    exp(r, k, 1)
                if in2:
                    relu(r + 2, (k + 2) % 4)
                    if i == -2:
                        mask_means()
                if ago2:
                    c_out(r - 2, (k + 2) % 4)
                if now:
                    tanh(r, k, 2)
                    tanh(r, k, 3)
                    exp(r, k, 2)
                    exp(r, k, 3)

            run(act, body)

        @block.vector
        def _(dve):
            count = [0]

            def link(ins):
                count[0] += 1
                ins.then_inc(dve_setup, 1)
                dve.wait_ge(dve_setup, count[0])

            def largest(name, ap, to, found):
                dve.wait_ge(loaded[name], 16)
                nc.vector.tensor_reduce(to, ap, AX.X, ALU.max, apply_absolute_value=True).then_inc(found, 1)

            def power(src, n, w):
                link(nc.vector.tensor_scalar(step_of[:, n:n + w], src, TINY, None, ALU.max))
                link(nc.vector.tensor_scalar(step_of[:, n:n + w].bitcast(i32), step_of[:, n:n + w].bitcast(i32),
                                             EXPONENT_BITS, None, ALU.bitwise_and))
                link(nc.vector.reciprocal(inv_step[:, n:n + w], step_of[:, n:n + w]))
                link(nc.vector.tensor_scalar(inv_step[:, n:n + w], inv_step[:, n:n + w], LIFT, None, ALU.mult))

            def split(hi, lo, ap, scale):
                link(nc.vector.tensor_scalar(hi, ap, scale, None, ALU.mult))
                return nc.vector.scalar_tensor_tensor(lo, ap, scale, hi, ALU.mult, ALU.subtract)

            def prepare_table():
                dve.wait_ge(amax_spread, 1)
                link(nc.vector.tensor_scalar(step_of[:, 0:2], amax_all[:, 0:2], 1.0 / QMAX, None, ALU.mult))
                link(nc.vector.reciprocal(inv_step[:, 0:2], step_of[:, 0:2]))
                nc.vector.tensor_tensor(h_scale[:, :], step_of[:, 0:1], step_of[:, 1:2], ALU.mult)
                link(nc.vector.tensor_scalar(conv_q[:, :], conv[:, :], inv_step[:, 1:2], ROUND, ALU.mult, ALU.add))
                nc.vector.tensor_scalar(emb_q[0:V, :], emb[0:V, :], inv_step[0:V, 0:1], ROUND, ALU.mult, ALU.add)
                link(nc.vector.tensor_scalar(conv_q[:, :], conv_q[:, :], ROUND, None, ALU.subtract))
                taps = conv_q[:, :].rearrange("p (d k) -> p k d", k=2)
                for tap in range(2):
                    last = nc.vector.scalar_tensor_tensor(table[0:V, tap, :], emb_q[0:V, :], ROUND, taps[0:V, tap, :],
                                                          ALU.subtract, ALU.mult)
                link(last)
                link(nc.vector.tensor_copy(table_hi[0:V, :, :], table[0:V, :, :]))
                nc.vector.tensor_tensor(table_lo[0:V, :, :], table[0:V, :, :], table_hi[0:V, :, :], ALU.subtract)\
                  .then_inc(table_ready, 1)

            def prepare_attention():
                dve.wait_ge(amax_spread, 2)
                power(amax2_all[:, :], 2, 2)
                nc.vector.tensor_scalar(unscale[:, 2:3], step_of[:, 2:3], 1.0 / (LIFT * LIFT * LIFT * PROJ_SCALE),
                                        None, ALU.mult)
                nc.vector.tensor_scalar(unscale[:, 3:4], step_of[:, 3:4], 1.0 / (LIFT * LIFT), None, ALU.mult)
                split(attn_hi[:, :], attn_lo[:, :], attn_w[:, :], inv_step[:, 2:3]).then_inc(attn_ready, 1)

            def prepare_gate():
                dve.wait_ge(means_mm, 3)
                nc.vector.tensor_copy(router_gamma[:, :], ps_b[:, 0:E])
                nc.vector.tensor_copy(gam[:, :], ps_b[:, E:2 * E])
                dve.wait_ge(consts_made, 2)
                nc.vector.tensor_tensor(gam_of[:, :], ps_b[0:E, P:2 * P], own_column[:, :], ALU.mult)\
                  .then_inc(gam_masked, 1)
                split(gate_hi[:, :], gate_lo[:, :], gate_w[:, :], inv_step[:, 3:4]).then_inc(gate_ready, 1)

            def scale_experts():
                dve.wait_ge(loaded["expert"], 16)
                link(nc.vector.tensor_tensor(expert_w[:, :, :], expert_w[:, :, :],
                                             gam[:, :].unsqueeze(2).to_broadcast([P, E, D]), ALU.mult))
                nc.vector.tensor_reduce(amax3[:, 0:1], expert_w[:, :, :], AX.XY, ALU.max,
                                        apply_absolute_value=True).then_inc(amax3_found, 1)

            def measure_bias():
                dve.wait_ge(means_mm, 4)
                link(nc.vector.tensor_copy(bias_row[:, :], ps_y[0][:, 0:D]))
                nc.vector.tensor_reduce(amax3[:, 1:2], bias_row[:, :], AX.X, ALU.max,
                                        apply_absolute_value=True).then_inc(amax3_found, 1)
                nc.vector.tensor_reduce(is_lo[:, :], lo_rows[:, :, :], AX.XY, ALU.max)

            def prepare_experts():
                dve.wait_ge(amax_spread, 3)
                power(amax3_all[:, :], 4, 2)
                nc.vector.tensor_scalar(unscale[:, 4:5], step_of[:, 4:5], 1.0 / (LIFT * LIFT * LIFT), None, ALU.mult)
                nc.vector.tensor_scalar(unscale[:, 5:6], step_of[:, 5:6], 1.0 / (LIFT * LIFT), None, ALU.mult)
                split(expert_hi[:, :, :], expert_lo[:, :, :], expert_w[:, :, :], inv_step[:, 4:5])

            def prepare_bias():
                link(split(bias_hi[:, :], bias_lo[:, :], bias_row[:, :], inv_step[:, 5:6]))
                link(nc.vector.tensor_scalar(is_hi[:, :], is_lo[:, :], -1.0, 1.0, ALU.mult, ALU.add))
                link(nc.vector.tensor_scalar(bias_hi[:, :], bias_hi[:, :], is_hi[:, 0:1], None, ALU.mult))
                link(nc.vector.scalar_tensor_tensor(bias_hi[:, :], bias_lo[:, :], is_lo[:, 0:1], bias_hi[:, :],
                                                    ALU.mult, ALU.add))
                for j in range(J):
                    rows = slice(32 * j, 32 * (j + 1))
                    last = nc.vector.tensor_copy(bias_blocks[rows, j, :], bias_hi[rows, :])
                last.then_inc(experts_ready, 1)

            nc.vector.memset(warm[:, :], 0.0).then_inc(warm_made, 1)
            dve.wait_ge(amax_zeroed, 1)
            largest("emb", emb[0:V, :], amax[0:V, 0:1], amax_found)
            largest("conv", conv[:, :], amax[:, 1:2], amax_found)
            largest("attn", attn_w[:, :], amax2[:, 0:1], amax2_found)
            largest("gate", gate_w[:, :], amax2[:, 1:2], amax2_found)


            def body(i, r, k):
                def one_hot(b, q):
                    if i is not None and b == 0:
                        dve.wait_ge(tokens_made, 1)
                    dve.wait_ge(y_loaded[q], 4 * (b - q) + 16)
                    if late(i, b, 2):
                        dve.wait_ge(h_mm, b - 1)
                    nc.vector.tensor_scalar(onehot[q % 2][0:V, 1:S + 1], y_bc[q][0:V, :], float(V - 1),
                                            vocab_id[0:V, 0:1], ALU.min, ALU.is_equal).then_inc(onehot_ready, 1)

                def aggregate(stats, mv, js, st_sem, mv_sem, at, lane):
                    dve.wait_ge(st_sem, at)
                    nc.vector.memset(idle[:, lane:lane + 1], 0.0)
                    for j in js:
                        last = nc.vector.bn_aggr(mv[:, j, :], stats[:, j, :])
                    last.then_inc(mv_sem, 1)

                def aggregate_1(b, q):
                    aggregate(stats1, mv1, range(J), st1_done, mv1_done, b + 1, 2)

                def aggregate_2(b, q, o):
                    aggregate(stats2, mv2, range(2 * o, 2 * o + 2), st2_done, mv2_done, b * 2 + o + 1, o)

                def stats_1(b, q, j):
                    if j == 0:
                        dve.wait_ge(h_relu, b + 1)
                    ins = nc.vector.bn_stats(stats1[:, j, :], h1[q][:, j, :])
                    if j == J - 1:
                        ins.then_inc(st1_done, 1)

                def shift_1(b, q):
                    dve.wait_ge(rstd1_done, b + 1)
                    nc.vector.scalar_tensor_tensor(shift1[:, :], mv1[:, :, 0], -1.0, rstd1[:, :], ALU.mult, ALU.mult)\
                      .then_inc(shift1_done, 1)

                def u1_lo(b, q):
                    dve.wait_ge(uthi_done, b + 1)
                    nc.vector.scalar_tensor_tensor(uT_lo[:, :], ps_a[:, :], LIFT, uT_hi[:, :],
                                                   ALU.mult, ALU.subtract).then_inc(utlo_done, 1)

                def p_lo(b, q):
                    dve.wait_ge(phi_done, b + 1)
                    nc.vector.scalar_tensor_tensor(pT_lo[:, :], ps_a[:, :], PROJ_SCALE, pT_hi[:, :],
                                                   ALU.mult, ALU.subtract).then_inc(plo_done, 1)

                def invert_sums(b, q, o):
                    dve.wait_ge(o_mm, b * 2 + o + 1)
                    nc.vector.reciprocal(inv_z[:, o, :], ps_o[o][:, D::O_STEP]).then_inc(invz_done, 1)

                def residual(b, q, o):
                    dve.wait_ge(invz_done, b * 2 + o + 1)
                    for n in range(2):
                        j = 2 * o + n
                        last = nc.vector.scalar_tensor_tensor(
                            h2[q % 2][:, j, :], ps_o[o][:, n * O_STEP:n * O_STEP + D], inv_z[:, o, n:n + 1],
                            h1[q][:, j, :], ALU.mult, ALU.add)
                    last.then_inc(h2_done, 1)

                def stats_2(b, q, o):
                    dve.wait_ge(h2_done, b * 2 + o + 1)
                    for j in range(2 * o, 2 * o + 2):
                        last = nc.vector.bn_stats(stats2[:, j, :], h2[q % 2][:, j, :])
                    last.then_inc(st2_done, 1)

                def norm_2(b, q):
                    dve.wait_ge(rstd2_done, b + 1)
                    if late(i, b):
                        dve.wait_ge(u2_mm, b)
                    for j in range(J):
                        last = nc.vector.tensor_scalar(u2[:, j, :], h2[q % 2][:, j, :], mv2[:, j, 0:1],
                                                       rstd2[:, j:j + 1], ALU.subtract, ALU.mult)
                    last.then_inc(u2_done, 1)

                def u2_lo(b, q):
                    dve.wait_ge(u2hi_done, b + 1)
                    nc.vector.scalar_tensor_tensor(u2T_lo[q % 2][:, :], ps_b[:, :], LIFT, u2T_hi[q % 2][:, :],
                                                   ALU.mult, ALU.subtract).then_inc(u2lo_done, 1)

                def over(x):
                    return x[:, :].unsqueeze(2).to_broadcast([P, J, E])

                def routing(b, q, n):
                    if n > 1:
                        dve.wait_ge(route, b * RD + n - 1)
                    if n == 1:
                        dve.wait_ge(g_mm, b + 1)
                        ins = nc.vector.scalar_tensor_tensor(
                            logits[:, :, :], ps_b[:, 0:J * E].rearrange("p (j e) -> p j e", j=J), unscale[:, 3:4],
                            router_gamma[:, :].unsqueeze(1).to_broadcast([P, J, E]), ALU.mult, ALU.add)
                    elif n == 2:
                        ins = nc.vector.tensor_reduce(top1[:, :], logits[:, :, :], AX.X, ALU.max)
                    elif n == 3:
                        ins = nc.vector.tensor_tensor(below[:, :, :], logits[:, :, :], over(top1), ALU.subtract)
                    elif n == 4:
                        ins = nc.vector.scalar_tensor_tensor(rank1[:, :, :], below[:, :, :], 0.0, first_wins[:, :, :],
                                                             ALU.is_equal, ALU.mult)
                    elif n == 5:
                        ins = nc.vector.tensor_reduce(best1[:, :], rank1[:, :, :], AX.X, ALU.max)
                    elif n == 6:
                        ins = nc.vector.tensor_tensor(pick1[:, :, :], rank1[:, :, :], over(best1), ALU.is_equal)
                    elif n == 7:
                        ins = nc.vector.scalar_tensor_tensor(rest[:, :, :], pick1[:, :, :], MASKED, below[:, :, :],
                                                             ALU.mult, ALU.add)
                    elif n == 8:
                        ins = nc.vector.tensor_reduce(top2[:, :], rest[:, :, :], AX.X, ALU.max)
                    elif n == 9:
                        ins = nc.vector.tensor_tensor(tied2[:, :, :], rest[:, :, :], over(top2), ALU.is_equal)
                    elif n == 10:
                        ins = nc.vector.tensor_tensor(rank2[:, :, :], tied2[:, :, :], first_wins[:, :, :], ALU.mult)
                    elif n == 11:
                        ins = nc.vector.tensor_reduce(best2[:, :], rank2[:, :, :], AX.X, ALU.max)
                    else:
                        ins = nc.vector.tensor_tensor(pick2[:, :, :], rank2[:, :, :], over(best2), ALU.is_equal)
                    ins.then_inc(route, 1)

                def softmax_sum(b, q):
                    dve.wait_ge(gexp_done, b + 1)
                    nc.vector.tensor_reduce(expo_sum[:, :], expo[:, :, :], AX.X, ALU.add).then_inc(zsum_done, 1)

                def softmax_inv(b, q):
                    dve.wait_ge(zsum_done, b + 1)
                    nc.vector.reciprocal(expo_inv[:, :], expo_sum[:, :]).then_inc(inv_done, 1)

                def start_acc(b, q):
                    dve.wait_ge(b_mm, b + 1)
                    if late(i, b, 2):
                        dve.wait_ge(fin_done, (b - 1) * J)
                    nc.vector.scalar_tensor_tensor(acc[q % 2][:, :, :].rearrange("p j d -> p (j d)"), ps_b[:, :],
                                                   unscale[:, 5:6], h2[q % 2][:, :, :].rearrange("p j d -> p (j d)"),
                                                   ALU.mult, ALU.add).then_inc(acc_init, 1)

                def add_expert(b, q, j, e):
                    if e == 0:
                        if j == 0:
                            dve.wait_ge(acc_init, b + 1)
                            dve.wait_ge(route_p, b * RP + RP)
                        dve.wait_ge(y_even_mm, b * J + j + 1)
                    else:
                        dve.wait_ge(acc_step, (b * J + j) * HE + e)
                    nc.vector.scalar_tensor_tensor(acc[q % 2][:, j, :], y_bank(i, b, j, 0)[:, e * D:(e + 1) * D],
                                                   combine_y[q % 2][:, j, e:e + 1], acc[q % 2][:, j, :],
                                                   ALU.mult, ALU.add).then_inc(acc_step, 1)

                ago4, ago3, ago2, ago1, now, in1, in3 = (has(i, n) for n in (-4, -3, -2, -1, 0, 1, 3))
                if ago4:
                    add_expert(r - 4, k, 3, 0)
                    add_expert(r - 4, k, 3, 1)
                if in3:
                    one_hot(r + 3, (k + 3) % 4)
                    if i == -3:
                        prepare_table()
                        prepare_attention()
                if ago4:
                    add_expert(r - 4, k, 3, 2)
                    add_expert(r - 4, k, 3, 3)
                if ago2:
                    norm_2(r - 2, (k + 2) % 4)
                if ago3:
                    start_acc(r - 3, (k + 1) % 4)
                if in1:
                    stats_1(r + 1, (k + 1) % 4, 0)
                if ago3:
                    add_expert(r - 3, (k + 1) % 4, 0, 0)
                if in1:
                    stats_1(r + 1, (k + 1) % 4, 1)
                if ago3:
                    add_expert(r - 3, (k + 1) % 4, 0, 1)
                if in1:
                    stats_1(r + 1, (k + 1) % 4, 2)
                if ago3:
                    add_expert(r - 3, (k + 1) % 4, 0, 2)
                if in1:
                    stats_1(r + 1, (k + 1) % 4, 3)
                if ago3:
                    add_expert(r - 3, (k + 1) % 4, 0, 3)
                if ago2:
                    u2_lo(r - 2, (k + 2) % 4)
                if in1:
                    aggregate_1(r + 1, (k + 1) % 4)
                    if i == -1:
                        prepare_gate()
                if now:
                    u1_lo(r, k)
                if ago3:
                    add_expert(r - 3, (k + 1) % 4, 1, 0)
                if ago2:
                    routing(r - 2, (k + 2) % 4, 1)
                if ago3:
                    add_expert(r - 3, (k + 1) % 4, 1, 1)
                if ago2:
                    routing(r - 2, (k + 2) % 4, 2)
                if ago3:
                    add_expert(r - 3, (k + 1) % 4, 1, 2)
                if ago2:
                    routing(r - 2, (k + 2) % 4, 3)
                if ago1:
                    invert_sums(r - 1, (k + 3) % 4, 0)
                if ago2:
                    routing(r - 2, (k + 2) % 4, 4)
                if ago3:
                    add_expert(r - 3, (k + 1) % 4, 1, 3)
                if ago2:
                    routing(r - 2, (k + 2) % 4, 5)
                    softmax_sum(r - 2, (k + 2) % 4)
                if in1:
                    shift_1(r + 1, (k + 1) % 4)
                    if i == -1:
                        scale_experts()
                if ago2:
                    routing(r - 2, (k + 2) % 4, 6)
                if ago1:
                    residual(r - 1, (k + 3) % 4, 0)
                if ago2:
                    routing(r - 2, (k + 2) % 4, 7)
                if now:
                    p_lo(r, k)
                    if i == 0:
                        measure_bias()
                        prepare_experts()
                        prepare_bias()
                if ago2:
                    routing(r - 2, (k + 2) % 4, 8)
                    softmax_inv(r - 2, (k + 2) % 4)
                    routing(r - 2, (k + 2) % 4, 9)
                if ago3:
                    add_expert(r - 3, (k + 1) % 4, 2, 0)
                if ago2:
                    routing(r - 2, (k + 2) % 4, 10)
                if ago3:
                    add_expert(r - 3, (k + 1) % 4, 2, 1)
                if ago2:
                    routing(r - 2, (k + 2) % 4, 11)
                if ago1:
                    invert_sums(r - 1, (k + 3) % 4, 1)
                if ago3:
                    add_expert(r - 3, (k + 1) % 4, 2, 2)
                if ago2:
                    routing(r - 2, (k + 2) % 4, 12)
                if ago1:
                    residual(r - 1, (k + 3) % 4, 1)
                if ago3:
                    add_expert(r - 3, (k + 1) % 4, 2, 3)
                if ago1:
                    stats_2(r - 1, (k + 3) % 4, 0)
                    stats_2(r - 1, (k + 3) % 4, 1)
                    aggregate_2(r - 1, (k + 3) % 4, 0)
                    aggregate_2(r - 1, (k + 3) % 4, 1)

            run(dve, body)

        @block.gpsimd
        def _(pool):
            count = [0]

            def link(ins):
                count[0] += 1
                ins.then_inc(pool_setup, 1)
                pool.wait_ge(pool_setup, count[0])

            nc.gpsimd.memset(amax[:, :], 0.0).then_inc(amax_zeroed, 1)
            nc.gpsimd.memset(sixteenth[:, :], 1.0 / NI)
            link(nc.gpsimd.memset(ident[:, :], 0.0))
            nc.gpsimd.affine_select(out=ident[:, :], in_=ident[:, :], compare_op=ALU.not_equal, fill=1.0, base=0,
                                    pattern=[[-1, P]], channel_multiplier=1).then_inc(consts_made, 1)
            nc.gpsimd.iota(vocab_id[:, :], pattern=[[0, 1]], base=0, channel_multiplier=1,
                           allow_small_or_imprecise_dtypes=True)
            for n in range(2):
                last = nc.gpsimd.memset(onehot[n][:, 0:1], 0.0)
            last.then_inc(tokens_made, 1)
            pool.wait_ge(amax_found, 2)
            nc.gpsimd.partition_all_reduce(amax_all[:, :], amax[:, :], P, ABSMAX).then_inc(amax_spread, 1)
            nc.gpsimd.memset(eps[:, :], EPS)
            nc.gpsimd.memset(minus_half[:, :], -0.5)
            nc.gpsimd.memset(lift[:, :], LIFT)
            nc.gpsimd.memset(column_of[:, :, :], 0.0)
            link(nc.gpsimd.memset(own_column[:, :], 0.0))
            pool.wait_ge(amax2_found, 2)
            nc.gpsimd.partition_all_reduce(amax2_all[:, :], amax2[:, :], P, ABSMAX).then_inc(amax_spread, 1)
            nc.gpsimd.affine_select(out=column_of[:, :, :], in_=column_of[:, :, :], compare_op=ALU.not_equal,
                                    fill=1.0, base=0, pattern=[[1, E], [0, P // E], [-1, E]], channel_multiplier=0)
            nc.gpsimd.affine_select(out=own_column[:, :], in_=own_column[:, :], compare_op=ALU.not_equal,
                                    fill=1.0, base=0, pattern=[[0, P // E], [-1, E]], channel_multiplier=1)
            link(nc.gpsimd.memset(lo_rows[:, :, :], 0.0))
            nc.gpsimd.affine_select(out=lo_rows[:, :, :], in_=lo_rows[:, :, :], compare_op=ALU.not_equal,
                                    fill=1.0, base=-16, pattern=[[-32, J], [-1, 16]], channel_multiplier=1)
            nc.gpsimd.tensor_copy(ident16[:, :], ident[:, :])
            nc.gpsimd.iota(first_wins[:, :, :], pattern=[[0, J], [-1, E]], base=E, channel_multiplier=0,
                           allow_small_or_imprecise_dtypes=True)
            nc.gpsimd.memset(cpack[:, :, :], 0.0)
            for n in range(4):
                nc.gpsimd.memset(u1[n][:, :, D:D + 4], 1.0)
            nc.gpsimd.memset(bias_blocks[:, :, :], 0.0).then_inc(consts_made, 1)
            pool.wait_ge(consts_made, 2)

            def spread_experts():
                pool.wait_ge(amax3_found, 2)
                nc.gpsimd.partition_all_reduce(amax3_all[:, :], amax3[:, :], P, ABSMAX).then_inc(amax_spread, 1)

            def body(i, r, k):
                def rstd(mv, var, rs, mv_sem, at, var_sem, rs_sem, b):
                    pool.wait_ge(mv_sem, at)
                    nc.gpsimd.tensor_tensor(var[:, :], mv[:, :, 1], eps[:, :], ALU.add)\
                      .then_inc(var_sem, 1)
                    pool.wait_ge(var_sem, b + 1)
                    nc.gpsimd.tensor_tensor(rs[:, :], var[:, :], minus_half[:, :], ALU.pow).then_inc(rs_sem, 1)

                def rstd_1(b, q):
                    rstd(mv1, var1, rstd1, mv1_done, b + 1, var1_done, rstd1_done, b)

                def rstd_2(b, q):
                    rstd(mv2, var2, rstd2, mv2_done, b * 2 + 2, var2_done, rstd2_done, b)

                def combine_weights(b, q):
                    if i is not None and b == 0:
                        pool.wait_ge(experts_ready, 1)
                    at = [0]

                    def step(ins):
                        at[0] += 1
                        ins.then_inc(route_p, 1)
                        pool.wait_ge(route_p, b * RP + at[0])

                    def over(x):
                        return x.unsqueeze(2).to_broadcast([P, J, E])

                    pool.wait_ge(route, b * RD + 12)
                    step(nc.gpsimd.tensor_tensor(picks[:, :, :], pick1[:, :, :], pick2[:, :, :], ALU.add))
                    pool.wait_ge(gexp_done, b + 1)
                    step(nc.gpsimd.tensor_tensor(picked[:, :, :], picks[:, :, :], expo[:, :, :], ALU.mult))
                    pool.wait_ge(inv_done, b + 1)
                    step(nc.gpsimd.tensor_tensor(inv_lift[:, :], expo_inv[:, :], lift[:, :], ALU.mult))
                    step(nc.gpsimd.tensor_tensor(combine[:, :, :], picked[:, :, :], over(inv_lift[:, :]), ALU.mult))
                    if late(i, b):
                        pool.wait_ge(ct_mm, b)
                    step(nc.gpsimd.tensor_tensor(
                        cpack[:, :, :].rearrange("p j (h e) -> p j h e", h=2)[:, :, :, 0:E],
                        picked[:, :, :].unsqueeze(2).to_broadcast([P, J, 2, E]),
                        inv_lift[:, :].unsqueeze(2).unsqueeze(3).to_broadcast([P, J, 2, E]), ALU.mult))
                    step(nc.gpsimd.tensor_tensor(cpack[:, :, E:2 * E], combine[:, :, :], cpack[:, :, 0:E],
                                                 ALU.subtract))
                    if late(i, b, 2):
                        pool.wait_ge(acc_step, (b - 1) * J * HE)
                    step(nc.gpsimd.tensor_tensor(combine_y[q % 2][:, :, :], combine[:, :, :],
                                                 unscale[:, 4:5].unsqueeze(2).to_broadcast([P, J, E]), ALU.mult))

                def sum_odd(b, q, j):
                    at = (b * J + j) * 2
                    pool.wait_ge(y_odd_done, b * J + j + 1)
                    y = y_odd[j % 2]
                    nc.gpsimd.tensor_tensor(sum2[j % 2][:, :, :], y[:, 0:2, :], y[:, 2:4, :], ALU.add)\
                      .then_inc(y_sum, 1)
                    pool.wait_ge(y_sum, at + 1)
                    nc.gpsimd.tensor_tensor(sum1[j % 2][:, :], sum2[j % 2][:, 0, :], sum2[j % 2][:, 1, :], ALU.add)\
                      .then_inc(y_sum, 1)

                def finish(b, q, j):
                    pool.wait_ge(y_sum, (b * J + j + 1) * 2)
                    pool.wait_ge(acc_step, (b * J + j + 1) * HE)
                    if j == 0 and late(i, b, 2):
                        pool.wait_ge(out_stored[q % 2], 8 * (b - q % 2))
                    nc.gpsimd.tensor_tensor(out_sb[q % 2][:, j, :], acc[q % 2][:, j, :], sum1[j % 2][:, :], ALU.add)\
                      .then_inc(fin_done, 1)

                ago4, ago3, ago2, ago1, in2 = (has(i, n) for n in (-4, -3, -2, -1, 2))
                if ago4:
                    finish(r - 4, k, 3)
                if ago3:
                    sum_odd(r - 3, (k + 1) % 4, 1)
                if ago2:
                    combine_weights(r - 2, (k + 2) % 4)
                if ago1:
                    rstd_2(r - 1, (k + 3) % 4)
                if ago3:
                    finish(r - 3, (k + 1) % 4, 0)
                    finish(r - 3, (k + 1) % 4, 1)
                    sum_odd(r - 3, (k + 1) % 4, 2)
                    sum_odd(r - 3, (k + 1) % 4, 3)
                    finish(r - 3, (k + 1) % 4, 2)
                if ago2:
                    sum_odd(r - 2, (k + 2) % 4, 0)
                if in2:
                    rstd_1(r + 2, (k + 2) % 4)
                    if i == -1:
                        spread_experts()

            run(pool, body)


_INS = ['x', 'L0_tok_emb_weight', 'L0_tok_conv_weight', 'L0_attn_attention_weights', 'L0_ffn_Ins_tk',
        'L0_ffn_gate_w', 'L0_ffn_expert_w', 'L0_ffn_expert_b', 'L0_ffn_gamma_w', 'L0_ffn_beta_w', 'L0_ffn_rmod_w']


def kernel(**inputs):
    import numpy as _np
    import concourse.bacc as _bacc
    from concourse import mybir as _mybir
    from concourse.bass_utils import run_bass_kernel_spmd as _run

    nc = _bacc.Bacc("TRN2", target_bir_lowering=False, num_devices=1)
    arrays, args = {}, []
    for name in _INS:
        a = _np.ascontiguousarray(inputs[name])
        arrays[f"in_{name}_dram"] = a
        args.append(nc.dram_tensor(f"in_{name}_dram", a.shape, _mybir.dt.from_np(a.dtype), kind="ExternalInput").ap())
    batch, seq = inputs['x'].shape
    width = inputs['L0_tok_emb_weight'].shape[1]
    args.append(nc.dram_tensor("out_dram", (batch, seq, width), _mybir.dt.float32, kind="ExternalOutput").ap())
    tower_kernel(nc, *args)
    r = _run(nc, [arrays], core_ids=[0])
    return r.results[0]["out_dram"]
```
